# Optimizing a Trainium2 kernel written in Bass

```python
import numpy as np
import jax
import jax.numpy as jnp

def _softmax(x, axis=-1):
    return jax.nn.softmax(x, axis=axis)

def _gelu(x):
    return jax.nn.gelu(x, approximate=True)

def _silu(x):
    return jax.nn.silu(x)

def _sigmoid(x):
    return jax.nn.sigmoid(x)

def _layernorm(x, axis=-1, eps=1e-05):
    m = jnp.mean(x, axis=axis, keepdims=True)
    v = jnp.var(x, axis=axis, keepdims=True)
    return (x - m) / jnp.sqrt(v + eps)

def _scatter_add(tgt, idx, src, axis=0):
    return tgt.at[idx].add(src)

def _segment_sum(src, seg, n):
    return jax.ops.segment_sum(src, seg, n)
kernel_name = 'mk_gnn_ffn_d1_gnn_r16_01e7d6'

def setup_inputs(seed: int=0):
    np.random.seed(seed)
    _w = jnp.asarray

    def _rec_inputs():
        import jax
        import jax.numpy as jnp
        _gk = jax.random.key(seed)
        x = -0.0002117 + 1 * jax.random.normal(jax.random.fold_in(_gk, 1), (625, 512), jnp.float32)
        _s = jax.random.randint(jax.random.fold_in(_gk, 2), (5000,), 0, 625, jnp.int32)
        _d = jax.random.randint(jax.random.fold_in(_gk, 3), (5000,), 0, 625, jnp.int32)
        _loop = jnp.arange(625, dtype=jnp.int32)
        src = jnp.concatenate([_s, _d, _loop])
        dst = jnp.concatenate([_d, _s, _loop])
        _o = jnp.argsort(dst, stable=True)
        src = src[_o]
        dst = dst[_o]
        return (x, src, dst)
    x, src, dst = _rec_inputs()

    def _L0_gnn_setup():
        import jax, jax.numpy as jnp
        import numpy as np
        BN_EPS = 1e-05

        def batch_norm(h, gamma, beta):
            mu = jnp.mean(h, axis=0)
            var = jnp.var(h, axis=0)
            return (h - mu) * jax.lax.rsqrt(var + BN_EPS) * gamma + beta
        key = jax.random.key(seed)
        ks = jax.random.split(key, 6)
        N, E, dim = (3125, 100000, 512)
        hidden = dim * 2
        x = jax.random.normal(ks[0], (N, dim), dtype=jnp.float32)
        edge_index = jax.random.randint(ks[1], (2, E), 0, N, dtype=jnp.int64)
        s1 = 1.0 / np.sqrt(dim)
        s2 = 1.0 / np.sqrt(hidden)
        return {'x': x, 'edge_index': edge_index, 'eps': jnp.float32(0.0), 'W1': jax.random.uniform(ks[2], (dim, hidden), jnp.float32, -s1, s1), 'b1': jnp.zeros((hidden,), jnp.float32), 'g1': jnp.ones((hidden,), jnp.float32), 'be1': jnp.zeros((hidden,), jnp.float32), 'W2': jax.random.uniform(ks[3], (hidden, dim), jnp.float32, -s2, s2), 'b2': jnp.zeros((dim,), jnp.float32), 'g2': jnp.ones((dim,), jnp.float32), 'be2': jnp.zeros((dim,), jnp.float32)}
    _L0_gnn_all = _L0_gnn_setup()
    _L0_gnn_in = {k: v for k, v in _L0_gnn_all.items() if k in ('eps', 'W1', 'b1', 'g1', 'be1', 'W2', 'b2', 'g2', 'be2')}
    del _L0_gnn_all

    def _L0_ffn_setup():
        import jax, jax.numpy as jnp
        import numpy as np
        E = 64
        K = 6
        NS = 2
        D = 512
        F = 512

        def _swiglu_ffn(x, wg, wu, wd):
            return jax.nn.silu(x @ wg) * (x @ wu) @ wd
        key = jax.random.key(seed)
        ks = jax.random.split(key, 8)
        s = 0.02
        return {'hidden_states': jax.random.normal(ks[0], (2, 1024, D), dtype=jnp.float32), 'Wr': jax.random.normal(ks[1], (D, E), dtype=jnp.float32) * s, 'sWg': jax.random.normal(ks[2], (NS, D, F), dtype=jnp.float32) * s, 'sWu': jax.random.normal(ks[3], (NS, D, F), dtype=jnp.float32) * s, 'sWd': jax.random.normal(ks[4], (NS, F, D), dtype=jnp.float32) * s, 'Wg': jax.random.normal(ks[5], (E, D, F), dtype=jnp.float32) * s, 'Wu': jax.random.normal(ks[6], (E, D, F), dtype=jnp.float32) * s, 'Wd': jax.random.normal(ks[7], (E, F, D), dtype=jnp.float32) * s}
    _L0_ffn_all = _L0_ffn_setup()
    _L0_ffn_in = {k: v for k, v in _L0_ffn_all.items() if k in ('Wr', 'sWg', 'sWu', 'sWd', 'Wg', 'Wu', 'Wd')}
    del _L0_ffn_all
    return {'x': x, 'src': src, 'dst': dst, 'L0_gnn_eps': _L0_gnn_in['eps'], 'L0_gnn_W1': _L0_gnn_in['W1'], 'L0_gnn_b1': _L0_gnn_in['b1'], 'L0_gnn_g1': _L0_gnn_in['g1'], 'L0_gnn_be1': _L0_gnn_in['be1'], 'L0_gnn_W2': _L0_gnn_in['W2'], 'L0_gnn_b2': _L0_gnn_in['b2'], 'L0_gnn_g2': _L0_gnn_in['g2'], 'L0_gnn_be2': _L0_gnn_in['be2'], 'L0_ffn_Wr': _L0_ffn_in['Wr'], 'L0_ffn_sWg': _L0_ffn_in['sWg'], 'L0_ffn_sWu': _L0_ffn_in['sWu'], 'L0_ffn_sWd': _L0_ffn_in['sWd'], 'L0_ffn_Wg': _L0_ffn_in['Wg'], 'L0_ffn_Wu': _L0_ffn_in['Wu'], 'L0_ffn_Wd': _L0_ffn_in['Wd']}

def reference(x, src, dst, L0_gnn_eps, L0_gnn_W1, L0_gnn_b1, L0_gnn_g1, L0_gnn_be1, L0_gnn_W2, L0_gnn_b2, L0_gnn_g2, L0_gnn_be2, L0_ffn_Wr, L0_ffn_sWg, L0_ffn_sWu, L0_ffn_sWd, L0_ffn_Wg, L0_ffn_Wu, L0_ffn_Wd):
    import jax
    import jax.numpy as jnp

    def _L0_gnn_ref(x, edge_index, eps, W1, b1, g1, be1, W2, b2, g2, be2):
        import jax, jax.numpy as jnp
        import numpy as np
        BN_EPS = 1e-05

        def batch_norm(h, gamma, beta):
            mu = jnp.mean(h, axis=0)
            var = jnp.var(h, axis=0)
            return (h - mu) * jax.lax.rsqrt(var + BN_EPS) * gamma + beta
        N = x.shape[0]
        src, dst = (edge_index[0], edge_index[1])
        agg = jax.ops.segment_sum(x[src], dst, num_segments=N)
        h = (1.0 + eps) * x + agg
        h = jax.nn.relu(batch_norm(h @ W1 + b1, g1, be1))
        h = h @ W2 + b2
        h = jax.nn.relu(batch_norm(h, g2, be2))
        return x + h

    def _L0_ffn_ref(hidden_states, Wr, sWg, sWu, sWd, Wg, Wu, Wd):
        import jax, jax.numpy as jnp
        import numpy as np
        E = 64
        K = 6
        NS = 2
        D = 512
        F = 512

        def _swiglu_ffn(x, wg, wu, wd):
            return jax.nn.silu(x @ wg) * (x @ wu) @ wd
        B, S, d = hidden_states.shape
        x = hidden_states.reshape(-1, d)
        N = x.shape[0]
        shared = jnp.zeros_like(x)
        for e in range(NS):
            shared = shared + _swiglu_ffn(x, sWg[e], sWu[e], sWd[e])
        logits = x @ Wr
        probs = jax.nn.softmax(logits, axis=-1)
        top_w, top_i = jax.lax.top_k(probs, K)
        top_w = top_w / jnp.sum(top_w, axis=-1, keepdims=True)
        gate = jnp.zeros((N, E), dtype=x.dtype).at[jnp.arange(N)[:, None], top_i].set(top_w)
        routed = jnp.zeros_like(x)
        for e in range(E):
            routed = routed + _swiglu_ffn(x, Wg[e], Wu[e], Wd[e]) * gate[:, e:e + 1]
        out = (shared + routed + x).reshape(B, S, d)
        return out
    edge_index = jnp.stack([src, dst])
    x = x + _L0_gnn_ref(_layernorm(x, axis=-1), edge_index, L0_gnn_eps, L0_gnn_W1, L0_gnn_b1, L0_gnn_g1, L0_gnn_be1, L0_gnn_W2, L0_gnn_b2, L0_gnn_g2, L0_gnn_be2)
    x = x + _L0_ffn_ref(_layernorm(x, axis=-1)[None], L0_ffn_Wr, L0_ffn_sWg, L0_ffn_sWu, L0_ffn_sWd, L0_ffn_Wg, L0_ffn_Wu, L0_ffn_Wd)[0]
    return x

_drawn_inputs = setup_inputs


def setup_inputs(seed=0):
    import zlib

    import numpy as np

    out = dict(_drawn_inputs(seed))
    spreads = {'L0_gnn_b1': (0.0, 2.0),
     'L0_gnn_g1': (1.0, 0.2),
     'L0_gnn_be1': (0.0, 0.294),
     'L0_gnn_b2': (0.0, 2.0),
     'L0_gnn_g2': (1.0, 0.2),
     'L0_gnn_be2': (0.0, 0.1)}
    factors = {'L0_ffn_Wr': 8.0,
     'L0_ffn_Wg': 8.0,
     'L0_ffn_Wu': 8.0,
     'L0_ffn_Wd': 8.0,
     'L0_ffn_sWg': 8.0,
     'L0_ffn_sWu': 8.0,
     'L0_ffn_sWd': 8.0}
    for name, (base, spread) in spreads.items():
        noise = np.random.default_rng([zlib.crc32(name.encode()), seed]).standard_normal(out[name].shape)
        drawn = base * np.exp(spread * noise) if base else spread * noise
        out[name] = jnp.asarray(drawn.astype(out[name].dtype))
    for name, factor in factors.items():
        out[name] = (out[name] * factor).astype(out[name].dtype)
    return out
```

```python
import concourse.bass as bass
from concourse import mybir
from contextlib import ExitStack

f32 = mybir.dt.float32
f32r = mybir.dt.float32r
bf16 = mybir.dt.bfloat16
i16 = mybir.dt.int16
i32 = mybir.dt.int32
u32 = mybir.dt.uint32
ALU = mybir.AluOpType
ACT = mybir.ActivationFunctionType
AX = mybir.AxisListType


def gnn_moe_kernel(nc, x_in, src_in, dst_in, eps_in, W1, b1, g1, be1, W2, b2, g2, be2,
                   Wr, sWg, sWu, sWd, Wg, Wu, Wd, out):
    N, D = x_in.shape
    NE = src_in.shape[0]
    H = W1.shape[1]
    E = Wg.shape[0]
    NS = sWg.shape[0]
    TOPK = 6
    EPS = 1e-5
    P = 125
    T = N // P
    C = NE // P
    assert N == T * P and NE == C * P and D == 512 and H == 2 * D and E == 64
    KD = D // 128
    KH = H // 128
    U = 11
    CP = -(-C // U) * U
    HALF = 314
    NP = 2 * HALF
    CAP = 96
    TILES = -(-N // CAP)
    ROWS = TILES * CAP
    DUMMY = N
    TAB = DUMMY + CAP
    MAXOV = 128
    NR = 6
    NSH = NS * T
    ITEM0 = 4 + 3 * NS
    ITEMS = ITEM0 + 3 * E
    DT = D * 4

    ctx = ExitStack()
    with ctx:
        base = [-(-nc.sbuf_base // 64) * 64]

        def region(size):
            at = base[0]
            base[0] = at + -(-size // 64) * 64
            assert base[0] <= nc.sbuf_usable_end, base[0]
            return at

        class Region:
            def __init__(self, size):
                self.start, self.end = region(size), 0
                self.end = base[0]
                self.at = self.start

            def rewind(self):
                self.at = self.start

            def place(self, name, shape, dt):
                n = mybir.dt.size(dt)
                for s in shape[1:]:
                    n *= s
                t = nc.alloc_sbuf_tensor_at(name, shape, dt, offset=self.at)
                self.at += -(-n // 32) * 32
                assert self.at <= self.end, (name, self.at - self.end)
                return t

        rMisc = Region(11136 - 0)
        rX = Region(T * DT)
        rH0 = Region(T * DT)
        rAT = Region(T * N * 4)
        rHT = Region(2 * KD * NP * 4 + 64)
        rRaw = Region(2 * 8192)
        rWin = Region(CP * P * 2)
        rOh = Region(CP * N * 2)

        m = rMisc.place
        ident = m("ident", [128, 128], f32)
        iota16 = m("iota16", [128, N], i16)
        vrows = m("vrows", [3 * (KH + KD), 128], f32)
        vcols = m("vcols", [128, 3 * (KH + KD)], f32)
        ones_b = m("ones_b", [P, 128], bf16)
        zero_b = m("zero_b", [P, P], bf16)
        before = m("before", [P, P], bf16)
        ones_row = m("ones_row", [1, P], f32)
        eps_sb = m("eps_sb", [1, 1], f32)
        eps1 = m("eps1", [P, 1], f32)
        pidx = m("pidx", [128, 1], f32)
        blk_lo = m("blk_lo", [128, T], f32)
        blk_hi = m("blk_hi", [128, T], f32)
        steps = m("steps", [1, CP // U], f32)
        cnt_cmp = m("cnt_cmp", [1, T, CP // U], f32)
        cmin = m("cmin", [C, 1], f32)
        cmax = m("cmax", [C, 1], f32)
        touch = m("touch", [C, T], f32)
        fromend = m("fromend", [C, 1], f32)
        after = m("after", [C, 1], f32)
        bounds = m("bounds", [C, 2 * T], f32)
        bmax = m("bmax", [2 * T, 1], f32)
        brow = m("brow", [1, 2 * T], f32)
        blen = m("blen", [1, T], f32)
        brow_i = m("brow_i", [1, 2 * T], i32)
        dcol = m("dcol", [P, CP], f32)
        scol = m("scol", [P, CP], f32)
        st6 = m("st6", [128, T, 6], f32)
        mv = m("mv", [128, T, 2], f32)
        veps = m("veps", [128, T], f32)
        vroot = m("vroot", [128, T], f32)
        rstd = m("rstd", [128, T], f32)
        vtmp = m("vtmp", [128, T], f32)
        marks = m("marks", [1, T + 2], f32)
        bscale = m("bscale", [128, KH + KD], f32)
        bshift = m("bshift", [128, KH + KD], f32)
        ovrow = m("ovrow", [1, 2 * MAXOV + 1], i32)
        lidx = m("lidx", [CAP, 1], i32)
        gidx = [m(f"gidx{i}", [CAP, 1], i32) for i in range(2)]
        sidx = [m(f"sidx{i}", [CAP, 1], i32) for i in range(2)]
        wr_f = m("wr_f", [128, KD, E], f32)
        wr_hi = m("wr_hi", [128, KD, E], f32r)
        wr_lo = m("wr_lo", [128, KD, E], f32r)

        x_sb = rX.place("x_sb", [P, T, D], f32)
        h0 = rH0.place("h0", [P, T, D], f32)
        rH0.rewind()
        xn = rH0.place("xn", [P, T, D], f32)
        aT = [rAT.place(f"aT{i}", [P, T, P], f32) for i in range(2)]
        ablk = rAT.place("ablk", [P, N], f32)
        rAT.rewind()
        lpre = rAT.place("lpre", [E, ROWS, 2], f32)
        rAT.rewind()
        zb = rAT.place("zb", [128, 2, NP], f32)
        rAT.rewind()
        z2 = rAT.place("z2", [128, KD, NP], f32)
        rAT.rewind()
        prod = rAT.place("prod", [P, TOPK, T, E], f32)
        ltile = rAT.place("ltile", [E, CAP, 2], f32)
        ohk = rAT.place("ohk", [P, TOPK, T, E], bf16)
        hT_hi = rHT.place("hT_hi", [128, KD, NP], f32r)
        hT_lo = rHT.place("hT_lo", [128, KD, NP], f32r)
        rHT.rewind()
        xnT_hi = rHT.place("xnT_hi", [128, KD, NP], f32r)
        xnT_lo = rHT.place("xnT_lo", [128, KD, NP], f32r)
        raw = [rRaw.place(f"raw{i}", [128, KD, 512], f32) for i in range(2)]
        win = rWin.place("win", [P, CP, P], bf16)
        rWin.rewind()
        r1_hi = rWin.place("r1_hi", [128, KH, NP], f32r)
        rWin.rewind()
        hs = [rWin.place(f"hs{i}", [128, D], f32) for i in range(2)]
        ysb = [rWin.place(f"ysb{i}", [CAP, D], f32) for i in range(2)]
        hTj_hi = rWin.place("hTj_hi", [128, KD, 128], f32r)
        hTj_lo = rWin.place("hTj_lo", [128, KD, 128], f32r)
        oh = rOh.place("oh", [P, CP, N], bf16)
        rOh.rewind()
        dst_i = rOh.place("dst_i", [C, P], i32)
        rOh.rewind()
        raw += [rOh.place(f"raw{i}", [128, KD, 512], f32) for i in range(2, NR)]
        wt_hi = [rOh.place(f"wt_hi{i}", [128, KD, 512], f32r) for i in range(3)]
        wt_lo = [rOh.place(f"wt_lo{i}", [128, KD, 512], f32r) for i in range(3)]
        tail = rOh.at
        r1_lo = rOh.place("r1_lo", [128, KH, NP], f32r)
        rOh.at = tail
        xg = [rOh.place(f"xg{i}", [CAP, D], f32) for i in range(2)]
        xT_hi = [rOh.place(f"xT_hi{i}", [128, KD, CAP], f32r) for i in range(2)]
        xT_lo = [rOh.place(f"xT_lo{i}", [128, KD, CAP], f32r) for i in range(2)]
        lgT = rOh.place("lgT", [E, NP], f32)
        prob = rOh.place("prob", [P, T, E], f32)
        maskb = rOh.place("maskb", [P, T, E], bf16)
        slotv = rOh.place("slotv", [P, T, E], f32)
        top8 = rOh.place("top8", [P, T, 8], f32)
        top8i = rOh.place("top8i", [P, T, 8], u32)
        top8f = rOh.place("top8f", [P, T, 8], f32)
        psum1 = rOh.place("psum1", [P, 5, T], f32)
        dest = rOh.place("dest", [P, TOPK, T], f32)
        dest_i = rOh.place("dest_i", [P, TOPK * T], i32)
        pair = rOh.place("pair", [P, TOPK * T, 2], f32)
        extra = rOh.place("extra", [128, E], f32)
        incl = rOh.place("incl", [128, E], f32)
        one64 = rOh.place("one64", [128, E], f32)
        cmp64 = rOh.place("cmp64", [128, E], f32)
        prod64 = rOh.place("prod64", [128, E], f32)
        ocol = rOh.place("ocol", [128, 6], f32)
        idx_sb = rOh.place("idx_sb", [CAP, E], i32)
        gate_sb = rOh.place("gate_sb", [CAP, E], f32)
        lcol = rOh.place("lcol", [CAP, 2], f32)
        iota64 = rOh.place("iota64", [128, E], f32)
        rowoff = rOh.place("rowoff", [128, E], f32)
        rHT.rewind()
        src_i = rHT.place("src_i", [C, P], i32)
        dstf = rHT.place("dstf", [C, P], f32)
        srcf = rHT.place("srcf", [C, P], f32)
        zrows = rHT.place("zrows", [CAP, D], f32)
        dst_i = rHT.place("dst_i2", [C, P], i32)

        ps = ctx.enter_context(nc.psum_tensor("ps", [128, 8, 512], f32))

        x_tab = nc.dram_tensor("x_tab", [TAB, D], f32, kind="Internal").ap()
        out_tab = nc.dram_tensor("out_tab", [TAB, D], f32, kind="Internal").ap()
        slots = nc.dram_tensor("slots", [E * ROWS, 2], f32, kind="Internal").ap()

        def sem(name):
            return ctx.enter_context(nc.semaphore(name))

        s_edges, s_x, s_vec, s_eps, s_wr = (sem(n) for n in
                                            ("edges_in", "x_in", "vectors_in", "eps_in", "router_in"))
        s_raw = [sem(f"raw_in{i}") for i in range(NR)]
        s_pre = sem("prefilled")
        s_cst = sem("constants")
        s_v = sem("vector_step")
        s_a = sem("scalar_step")
        s_edgef, s_edgeT, s_bnd, s_bndT, s_bmx, s_bmxT, s_brow = (sem(n) for n in (
            "edges_float", "edges_T", "bounds", "bounds_T", "bounds_max", "bounds_row_T", "block_rows"))
        s_vecT, s_oh, s_win, s_adj, s_atc, s_at, s_h0 = (sem(n) for n in (
            "vectors_T", "onehot_src", "windows", "adjacency", "aT_copied", "aT_ready", "h0_ready"))
        s_ac, s_aT = sem("A_copied"), sem("A_transposed")
        s_agg, s_hhiT, s_hT = (sem(n) for n in ("aggregated", "hT_hi_ready", "hT_ready"))
        s_var, s_root = sem("variance"), sem("root")
        s_z, s_zc, s_sc, s_r, s_rhi, s_rlo = (sem(n) for n in (
            "z_product", "z_copied", "bn_scale", "relu_done", "relu_hi", "relu_lo"))
        s_h2T, s_x1 = sem("h2_T"), sem("x1_piece")
        s_xn, s_xnp, s_xnhi, s_xnlo = sem("xn_tile"), sem("xn_T"), sem("xnT_hi"), sem("xnT_lo")
        s_xtab, s_lgT, s_lgTc, s_lg = sem("x_tab_out"), sem("logits_T"), sem("logits_T_copied"), sem("logits")
        s_nmx, s_exp, s_mask, s_pos, s_dest = (sem(n) for n in ("neg_max", "exps", "mask", "positions", "dest"))
        s_sct, s_lst, s_lstT, s_idx = (sem(n) for n in ("slots_out", "slots_in", "slots_T", "index_ready"))
        s_ovc, s_ovT, s_ov = sem("extra_cols"), sem("extra_T"), sem("extra_ready")
        s_acc = sem("base_sum")
        s_hi, s_lo = sem("weights_hi"), sem("weights_lo")
        s_g, s_u, s_th, s_d, s_tx = (sem(n) for n in ("gate_product", "up_product", "h_T", "down_product", "x_T"))
        s_silu, s_mul, s_hhi, s_hlo, s_y = (sem(n) for n in ("silu_done", "h_done", "h_hi", "h_lo", "y_ready"))
        s_xg = [sem(f"x_gathered{i}") for i in range(2)]
        s_xhi, s_xlo = sem("x_hi"), sem("x_lo")
        s_col = sem("index_column")
        s_go = sem("indirect_let_through")
        s_tab, s_scat, s_lc, s_li, s_out = (sem(n) for n in (
            "out_tab_base", "y_added", "extra_slots_in", "extra_index", "out_done"))

        W1v = W1.rearrange("(k p) n -> p k n", p=128)
        W2v = W2.rearrange("(k p) n -> p k n", p=128)
        first = [W1v[:, :, 0:512], W1v[:, :, 512:1024], W2v[:, 0:KD, :], W2v[:, KD:KH, :]]
        for s in range(NS):
            first += [w[s].rearrange("(k p) n -> p k n", p=128) for w in (sWg, sWu, sWd)]
        experts = [w.rearrange("e (k p) n -> e p k n", p=128) for w in (Wg, Wu, Wd)]
        G_, U_, D_ = 1, 2, 0

        def item_g(j):
            return ITEM0 + 3 * j - 1

        def item_u(j):
            return ITEM0 + 3 * j

        def item_d(j):
            return ITEM0 + 3 * j + 4

        PAIRS = (E - 2) // 2
        item_end = ITEMS
        uses = [len([i for i in range(ITEMS) if i % NR == s]) for s in range(NR)]

        def item_of(r, j):
            return ITEM0 + 3 * j - 1 + r

        block = ctx.enter_context(nc.Block())

        @block.sync
        def _(sp):
            sp.dma_start(dst_i[:], dst_in.rearrange("(c p) -> c p", p=P)).then_inc(s_edges, 16)
            sp.dma_start(src_i[:], src_in.rearrange("(c p) -> c p", p=P)).then_inc(s_edges, 16)
            sp.dma_start(x_sb[:], x_in.rearrange("(t p) d -> p t d", p=P)).then_inc(s_x, 16)
            for i in range(2):
                sp.dma_start(raw[i][:], first[i]).then_inc(s_raw[i], 16)
            sp.wait_ge(s_adj, T)
            for i in range(2, ITEM0):
                if i >= NR:
                    sp.wait_ge(s_lo, i - NR + 1)
                sp.dma_start(raw[i % NR][:], first[i]).then_inc(s_raw[i % NR], 16)
                if i == NR - 1:
                    pass
            for r, i in ((0, ITEM0), (1, ITEM0 + 1)):
                sp.wait_ge(s_lo, i - NR + 1)
                sp.dma_start(raw[i % NR][:], experts[r][0]).then_inc(s_raw[i % NR], 16)

            def load_step(j, h):
                for r in range(3):
                    i = item_of(r, j)
                    slot = (ITEM0 - 1 + 3 * (1 + h) + r) % NR
                    sp.wait_ge(s_lo, i - NR + 1)
                    sp.dma_start(raw[slot][:], experts[r][j if r < 2 else j - 1]).then_inc(s_raw[slot], 16)

            load_step(1, 0)
            load_step(2, 1)
            with sp.Fori(1, PAIRS) as i:
                for h in range(2):
                    load_step(i * 2 + (1 + h), h)
            load_step(E - 1, 0)
            sp.wait_ge(s_lo, ITEMS - NR)
            sp.dma_start(raw[(ITEMS - 1) % NR][:], experts[2][E - 1]).then_inc(s_raw[(ITEMS - 1) % NR], 16)
            sp.wait_ge(s_ov, 1)
            total = sp.value_load(ovrow[0:1, 2 * MAXOV:2 * MAXOV + 1], min_val=0, max_val=MAXOV)
            with sp.If(total > 0):
                with sp.Fori(0, total) as o:
                    e = sp.value_load(ovrow[0:1, bass.ds(o, 1)], min_val=0, max_val=E - 1)
                    sp.wait_ge(s_lo, o * 3 + ITEMS)
                    for r in range(3):
                        sp.dma_start(raw[r][:], experts[r][e]).then_inc(s_raw[r], 16)
            sp.wait_ge(s_scat, total * 16 + 16 * E)
            sp.dma_start(out.rearrange("(a b) d -> a (b d)", b=5), out_tab[0:N, :].rearrange("(a b) d -> a (b d)", b=5)).then_inc(s_out, 16)
            sp.wait_ge(s_out, 16)

        @block.gpsimd
        def _(pool):
            g = nc.gpsimd
            g.iota(iota16[:], pattern=[[1, N]], base=0, channel_multiplier=0).then_inc(s_cst, 1)
            g.memset(ident[:], 0.0).then_inc(s_cst, 1)
            pool.wait_ge(s_cst, 2)
            g.affine_select(out=ident[:], in_=ident[:], compare_op=ALU.not_equal, fill=1.0, base=0,
                            pattern=[[-1, 128]], channel_multiplier=1).then_inc(s_cst, 1)
            imp = dict(allow_small_or_imprecise_dtypes=True)
            g.iota(pidx[:], pattern=[[0, 1]], base=0, channel_multiplier=1, **imp).then_inc(s_cst, 1)
            g.iota(blk_lo[:], pattern=[[P, T]], base=0, channel_multiplier=0, **imp).then_inc(s_cst, 1)
            g.iota(blk_hi[:], pattern=[[P, T]], base=P, channel_multiplier=0, **imp).then_inc(s_cst, 1)
            g.iota(steps[:], pattern=[[U, CP // U]], base=0, channel_multiplier=0, **imp).then_inc(s_cst, 1)
            g.memset(lpre[:], 0.0).then_inc(s_cst, 1)
            pool.wait_ge(s_cst, 8)
            g.iota(lpre[:, :, 0], pattern=[[0, TILES], [1, CAP]], base=DUMMY, channel_multiplier=0,
                   **imp).then_inc(s_cst, 1)
            g.memset(zrows[:], 0.0).then_inc(s_cst, 1)
            pool.wait_ge(s_cst, 10)
            g.dma_start(slots.rearrange("(e r) v -> e (r v)", r=ROWS),
                        lpre[:].rearrange("e r v -> e (r v)")).then_inc(s_pre, 16)
            g.dma_start(x_tab[DUMMY:TAB, :], zrows[:]).then_inc(s_pre, 16)
            g.dma_start(out_tab[DUMMY:TAB, :], zrows[:]).then_inc(s_pre, 16)
            g.memset(before[:], 1.0).then_inc(s_cst, 1)
            pool.wait_ge(s_cst, 11)
            g.affine_select(out=before[:], in_=before[:], compare_op=ALU.is_gt, fill=0.0, base=0,
                            pattern=[[1, P]], channel_multiplier=-1).then_inc(s_cst, 1)
            g.memset(ones_b[:], 1.0).then_inc(s_cst, 1)
            pool.wait_ge(s_xn, T)
            g.dma_start(x_tab[0:N, :].rearrange("(t p) d -> p t d", p=P), xn[:]).then_inc(s_xtab, 16)
            pool.wait_ge(s_z, KH + KD)
            g.iota(iota64[:], pattern=[[1, E]], base=0, channel_multiplier=0, **imp).then_inc(s_cst, 1)
            g.iota(rowoff[:], pattern=[[ROWS, E]], base=0, channel_multiplier=0, **imp).then_inc(s_cst, 1)
            g.iota(pair[:, :, 0].rearrange("p (k t) -> p k t", t=T), pattern=[[0, TOPK], [P, T]], base=0,
                   channel_multiplier=1, **imp).then_inc(s_cst, 1)
            pool.wait_ge(s_dest, 1)
            pool.wait_ge(s_cst, 16)
            pool.wait_ge(s_pre, 48)
            for n in range(TOPK * T):
                g.indirect_dma_start(out=slots, out_offset=bass.IndirectOffsetOnAxis(ap=dest_i[:, n:n + 1].bitcast(u32), axis=0),
                                     in_=pair[:, n, :], in_offset=None).then_inc(s_sct, 16)
            pool.wait_ge(s_sct, 16 * TOPK * T)
            g.dma_start(ltile[:], slots.rearrange("(e r) v -> e r v", r=ROWS)[:, 0:CAP, :]).then_inc(s_lst, 16)
            pool.wait_ge(s_xtab, 16)
            pool.wait_ge(s_idx, 1)

            def gather(j, h, copies):
                g.tensor_copy(gidx[h][:], idx_sb[:, bass.ds(j, 1)]).then_inc(s_col, 1)
                pool.wait_ge(s_col, copies)
                pool.sem_inc(s_go, 1)
                g.indirect_dma_start(out=xg[h][:], out_offset=None, in_=x_tab,
                                     in_offset=bass.IndirectOffsetOnAxis(ap=gidx[h][:].bitcast(u32), axis=0)
                                     ).then_inc(s_xg[h], 16)

            def scatter(j, h, copies):
                g.tensor_copy(sidx[h][:], idx_sb[:, bass.ds(j, 1)]).then_inc(s_col, 1)
                pool.wait_ge(s_col, copies)
                pool.wait_ge(s_y, j + (NSH + 1))
                if not isinstance(j, int) or j >= 1:
                    pool.wait_ge(s_scat, j * 16)
                pool.sem_inc(s_go, 1)
                g.indirect_dma_start(out=out_tab, out_offset=bass.IndirectOffsetOnAxis(ap=sidx[h][:].bitcast(u32), axis=0),
                                     in_=ysb[h][:], in_offset=None, compute_op=ALU.add).then_inc(s_scat, 16)

            gather(0, 0, 1)
            gather(1, 1, 2)
            pool.wait_ge(s_y, NSH)
            g.dma_start(out_tab[0:N, :].rearrange("(t p) d -> p t d", p=P), x_sb[:]).then_inc(s_tab, 16)
            pool.wait_ge(s_tab, 16)
            pool.wait_ge(s_tx, 1)
            gather(2, 0, 3)
            pool.wait_ge(s_tx, 2)
            gather(3, 1, 4)
            scatter(0, 0, 5)
            with pool.Fori(0, (E - 4) // 2) as i:
                for h in range(2):
                    pool.wait_ge(s_tx, i * 2 + (h + 3))
                    gather(i * 2 + (4 + h), h, i * 4 + (6 + 2 * h))
                    scatter(i * 2 + (1 + h), 1 - h, i * 4 + (7 + 2 * h))
            for j in range(E - 3, E):
                scatter(j, j % 2, E + j + 1)
            pool.wait_ge(s_scat, 16 * E)
            pool.wait_ge(s_ov, 1)
            total = pool.value_load(ovrow[0:1, 2 * MAXOV:2 * MAXOV + 1], min_val=0, max_val=MAXOV)
            with pool.If(total > 0):
                with pool.Fori(0, total) as o:
                    at = pool.value_load(ovrow[0:1, bass.ds(o + MAXOV, 1)], min_val=0, max_val=E * ROWS - CAP)
                    g.dma_start(lcol[:], slots[bass.ds(at, CAP), :]).then_inc(s_lc, 16)
                    pool.wait_ge(s_li, o + 1)
                    pool.sem_inc(s_go, 1)
                    g.indirect_dma_start(out=xg[0][:], out_offset=None, in_=x_tab,
                                         in_offset=bass.IndirectOffsetOnAxis(ap=lidx[:, 0:1].bitcast(u32), axis=0)
                                         ).then_inc(s_xg[0], 16)
                    pool.wait_ge(s_y, o + (NSH + E + 1))
                    pool.sem_inc(s_go, 1)
                    g.indirect_dma_start(out=out_tab, out_offset=bass.IndirectOffsetOnAxis(ap=lidx[:, 0:1].bitcast(u32), axis=0),
                                         in_=ysb[0][:], in_offset=None, compute_op=ALU.add).then_inc(s_scat, 16)
                    pool.wait_ge(s_scat, o * 16 + 16 * (E + 1))

        @block.scalar
        def _(act):
            sc = nc.scalar
            at = 0
            for v, k in ((b1, KH), (g1, KH), (be1, KH), (b2, KD), (g2, KD), (be2, KD)):
                act.dma_start(vrows[at:at + k, :], v.rearrange("(k p) -> k p", p=128)).then_inc(s_vec, 16)
                at += k
            act.dma_start(eps_sb[:], eps_in).then_inc(s_eps, 16)
            act.dma_start(wr_f[:], Wr.rearrange("(k p) e -> p k e", p=128)).then_inc(s_wr, 16)
            act.wait_ge(s_wr, 16)
            sc.activation(wr_hi[:], wr_f[:], ACT.Copy).then_inc(s_hi, 1)
            act.wait_ge(s_var, 1)
            sc.activation(vroot[0:P, :], veps[0:P, :], ACT.Sqrt).then_inc(s_root, 1)

            def split_hi(slot, n, use, buf):
                act.wait_ge(s_raw[slot], use)
                sc.activation(wt_hi[buf][:], raw[slot][:], ACT.Copy).then_inc(s_hi, 1)

            def a_copy(b):
                act.wait_ge(s_adj, b + 1)
                if b == 0:
                    act.wait_ge(s_pre, 48)
                else:
                    act.wait_ge(s_aT, b)
                q = 2 * (b % 2)
                sc.activation(ablk[:, 0:4 * P], ps[0:P, q, 0:4 * P], ACT.Copy).then_inc(s_ac, 1)
                sc.activation(ablk[:, 4 * P:N], ps[0:P, q + 1, 0:P], ACT.Copy).then_inc(s_ac, 1)

            def at_copy(b):
                act.wait_ge(s_aT, b + 1)
                if b >= 2:
                    act.wait_ge(s_agg, b - 1)
                sc.activation(aT[b % 2][:, 0:4, :], ps[0:P, 4, 0:4 * P].rearrange("p (s n) -> p s n", s=4),
                              ACT.Copy).then_inc(s_atc, 1)
                sc.activation(aT[b % 2][:, 4, :], ps[0:P, 7, 0:P], ACT.Copy).then_inc(s_atc, 1)

            def agg_hi(b):
                act.wait_ge(s_agg, b + 1)
                sc.activation(hT_hi[:, :, b * P:(b + 1) * P],
                              ps[:, 5, 0:KD * P].rearrange("p (k n) -> p k n", k=KD), ACT.Copy).then_inc(s_hhiT, 1)

            a_copy(0)
            for b in range(1, T):
                a_copy(b)
                at_copy(b - 1)
                if b >= 2:
                    agg_hi(b - 2)
            at_copy(T - 1)
            split_hi(0, 0, 16, 0)
            agg_hi(T - 2)
            split_hi(1, 1, 16, 1)
            agg_hi(T - 1)
            split_hi(2, 2, 16, 2)

            zn = [0]

            def z_copy(i, dst, bias):
                act.wait_ge(s_z, i + 1)
                q = 2 * (i % 2)
                sc.activation(dst.rearrange("p (h n) -> p h n", h=2), ps[:, q:q + 2, 0:HALF], ACT.Identity,
                              bias=vcols[:, bias:bias + 1]).then_inc(s_zc, 1)

            act.wait_ge(s_vecT, 2)
            act.wait_ge(s_at, T)
            act.wait_ge(s_agg, T)
            z_copy(0, zb[:, 0, :], 0)
            for f in range(KH):
                act.wait_ge(s_var, 2 + f)
                sc.activation(vroot[:, 0:1], veps[:, 0:1], ACT.Sqrt).then_inc(s_root, 1)
                if f + 1 < KH:
                    if f >= 1:
                        act.wait_ge(s_rlo, f)
                    z_copy(f + 1, zb[:, (f + 1) % 2, :], f + 1)
                act.wait_ge(s_sc, f + 1)
                sc.activation(zb[:, f % 2, :], zb[:, f % 2, :], ACT.Relu, bias=bshift[:, f:f + 1],
                              scale=bscale[:, f:f + 1]).then_inc(s_r, 1)
                act.wait_ge(s_r, f + 1)
                sc.activation(r1_hi[:, f, :], zb[:, f % 2, :], ACT.Copy).then_inc(s_rhi, 1)
                if f == 4:
                    act.wait_ge(s_z, 4)
                    split_hi(3, 3, 16, 0)
            act.wait_ge(s_z, KH)
            split_hi(4, 4, 16, G_)
            act.wait_ge(s_rlo, KH)
            z_copy(KH, z2[:, 0, :], 3 * KH)
            for d in range(KD):
                i = KH + d
                act.wait_ge(s_var, 2 + i)
                sc.activation(vroot[:, 0:1], veps[:, 0:1], ACT.Sqrt).then_inc(s_root, 1)
                if d + 1 < KD:
                    z_copy(i + 1, z2[:, d + 1, :], 3 * KH + d + 1)
                act.wait_ge(s_sc, i + 1)
                sc.activation(z2[:, d, :], z2[:, d, :], ACT.Relu, bias=bshift[:, i:i + 1],
                              scale=bscale[:, i:i + 1]).then_inc(s_r, 1)
            split_hi(5, 5, 16, U_)
            split_hi(0, 6, 32, D_)
            act.wait_ge(s_var, 2 + KH + KD)
            sc.activation(vroot[0:P, :], veps[0:P, :], ACT.Sqrt).then_inc(s_root, 1)
            for t in range(T):
                act.wait_ge(s_xnp, t + 1)
                sc.activation(xnT_hi[:, :, t * P:(t + 1) * P],
                              ps[:, t % 2, 0:KD * P].rearrange("p (k n) -> p k n", k=KD), ACT.Copy).then_inc(s_xnhi, 1)
            act.wait_ge(s_lgT, 1)
            sc.activation(lgT[:].rearrange("p (h n) -> p h n", h=2), ps[0:E, 2:4, 0:HALF], ACT.Copy).then_inc(s_lgTc, 1)
            act.wait_ge(s_nmx, 1)
            for t in range(T):
                sc.activation(prob[:, t, :], ps[0:P, 4, t * E:(t + 1) * E], ACT.Exp, bias=psum1[:, 0, t:t + 1],
                              accum_out=psum1[:, 1, t:t + 1]).then_inc(s_exp, 1)

            def silu(J, h, m_):
                act.wait_ge(s_g, J + 1)
                if not isinstance(J, int) or J >= 2:
                    act.wait_ge(s_th, J - 1)
                sc.activation(hs[h][0:m_, :], ps[0:m_, 0, :], ACT.Silu).then_inc(s_silu, 1)

            def h_hi(J, m_):
                act.wait_ge(s_th, J + 1)
                if not isinstance(J, int) or J >= 1:
                    act.wait_ge(s_d, J)
                sc.activation(hTj_hi[:, :, 0:m_], ps[:, 3, 0:KD * m_].rearrange("p (k n) -> p k n", k=KD),
                              ACT.Copy).then_inc(s_hhi, 1)

            for q in range(NSH):
                silu(q, q % 2, P)
                if q == T - 1:
                    split_hi(7 % NR, 7, 32, G_)
                if q == NSH - 1:
                    split_hi(ITEM0 % NR, ITEM0, 32, G_)
                if q >= 1:
                    h_hi(q - 1, P)
                if q == T - 1:
                    act.wait_ge(s_u, T)
                    split_hi(8 % NR, 8, 32, U_)
                if q == T:
                    act.wait_ge(s_d, T)
                    split_hi(9 % NR, 9, 32, D_)
                if q == NSH - 1:
                    act.wait_ge(s_u, NSH)
                    split_hi((ITEM0 + 1) % NR, ITEM0 + 1, 32, U_)
            def x_hi(j, h):
                act.wait_ge(s_tx, j + 1)
                if not isinstance(j, int) or j >= 2:
                    act.wait_ge(s_u, j + (NSH - 1))
                sc.activation(xT_hi[h][:], ps[:, 5, 0:KD * CAP].rearrange("p (k n) -> p k n", k=KD),
                              ACT.Copy).then_inc(s_xhi, 1)

            def y_copy(j, h, gate):
                act.wait_ge(s_d, j + (NSH + 1))
                if not isinstance(j, int) or j >= 2:
                    act.wait_ge(s_scat, j * 16 - 16)
                sc.activation(ysb[h][:], ps[0:CAP, 2, :], ACT.Copy, scale=gate).then_inc(s_y, 1)

            x_hi(0, 0)
            h_hi(NSH - 1, P)

            def raw_use(r, j, h):
                base_i = ITEM0 - 1 + 3 * (1 + h) + r
                return base_i % NR, (j - (1 + h)) * 8 + 16 * (base_i // NR + 1)

            def step(j, h, hn, first_=False, last_=False):
                J = j + NSH
                silu(J, h, CAP)
                if not first_:
                    h_hi(J - 1, CAP)
                if not last_:
                    x_hi(j + 1, hn)
                    slot, use = raw_use(0, j + 1, (h + 0) % 2)
                    split_hi(slot, 0, use, G_)
                    slot, use = raw_use(1, j + 1, h % 2)
                    act.wait_ge(s_u, J + 1)
                    split_hi(slot, 0, use, U_)
                    slot, use = raw_use(2, j + 1, h % 2)
                    act.wait_ge(s_d, J)
                    split_hi(slot, 0, use, D_)
                else:
                    act.wait_ge(s_d, J)
                    split_hi((ITEMS - 1) % NR, 0, 16 * uses[(ITEMS - 1) % NR], D_)
                if not first_:
                    y_copy(j - 1, hn, gate_sb[:, bass.ds(j - 1, 1)])

            step(0, 0, 1, first_=True)
            step(1, 1, 0)
            step(2, 0, 1)
            with act.Fori(0, PAIRS - 1) as i:
                step(i * 2 + 3, 1, 0)
                step(i * 2 + 4, 0, 1)
            step(E - 1, 1, 0, last_=True)
            h_hi(NSH + E - 1, CAP)
            y_copy(E - 1, 1, gate_sb[:, E - 1:E])
            act.wait_ge(s_ov, 1)
            total = act.value_load(ovrow[0:1, 2 * MAXOV:2 * MAXOV + 1], min_val=0, max_val=MAXOV)
            with act.If(total > 0):
                with act.Fori(0, total) as o:
                    for r, buf in enumerate((G_, U_, D_)):
                        act.wait_ge(s_raw[r], o * 16 + 16 * (uses[r] + 1))
                        act.wait_ge(s_d, o + (NSH + E))
                        sc.activation(wt_hi[buf][:], raw[r][:], ACT.Copy).then_inc(s_hi, 1)
                    x_hi(o + E, 0)
                    silu(o + (NSH + E), 0, CAP)
                    h_hi(o + (NSH + E), CAP)
                    act.wait_ge(s_scat, o * 16 + 16 * E)
                    y_copy(o + E, 0, lcol[:, 1:2])

        @block.vector
        def _(dve):
            v = nc.vector
            n_v = [0]

            def link(ins):
                n_v[0] += 1
                ins.then_inc(s_v, 1)
                dve.wait_ge(s_v, n_v[0])

            v.memset(dcol[:], -1.0)
            v.memset(scol[:], -1.0)
            v.memset(zero_b[:], 0.0)
            link(v.memset(ones_row[:], 1.0))
            dve.wait_ge(s_edges, 32)
            v.tensor_copy(dstf[:], dst_i[:]).then_inc(s_edgef, 1)
            v.tensor_copy(srcf[:], src_i[:]).then_inc(s_edgef, 1)
            dve.wait_ge(s_edgef, 2)
            v.tensor_reduce(cmin[:], dstf[:], axis=AX.X, op=ALU.min)
            link(v.tensor_reduce(cmax[:], dstf[:], axis=AX.X, op=ALU.max))
            dve.wait_ge(s_cst, 7)
            link(v.tensor_scalar(touch[:], blk_hi[0:C, :], cmin[:], None, ALU.is_gt))
            link(v.scalar_tensor_tensor(touch[:], blk_lo[0:C, :], cmax[:], touch[:], ALU.is_le, ALU.mult))
            v.tensor_scalar(fromend[:], pidx[0:C, :], -1.0, float(C), ALU.mult, ALU.add)
            link(v.tensor_scalar(after[:], pidx[0:C, :], 1.0, None, ALU.add))
            v.tensor_scalar(bounds[:, 0:T], touch[:], fromend[:], None, ALU.mult).then_inc(s_bnd, 1)
            v.tensor_scalar(bounds[:, T:2 * T], touch[:], after[:], None, ALU.mult).then_inc(s_bnd, 1)
            dve.wait_ge(s_edgeT, 1)
            v.tensor_copy(dcol[:, 0:C], ps[0:P, 6, 0:C])
            link(v.tensor_copy(scol[:, 0:C], ps[0:P, 6, C:2 * C]))

            def sources(a, b):
                for c in range(a, b):
                    v.tensor_scalar(oh[:, c, :], iota16[0:P, :], scol[:, c:c + 1], None, ALU.is_equal).then_inc(s_oh, 1)

            FIRST = 24
            sources(0, 9)
            dve.wait_ge(s_bndT, 1)
            v.tensor_reduce(bmax[:], ps[0:2 * T, 7, 0:C], axis=AX.X, op=ALU.max).then_inc(s_bmx, 1)
            sources(9, FIRST)
            dve.wait_ge(s_bmxT, 1)
            link(v.tensor_scalar(brow[:, 0:T], ps[0:1, 7, 128:128 + T], -1.0, float(C), ALU.mult, ALU.add))
            link(v.tensor_scalar(brow[:, 0:T], brow[:, 0:T], float(C - 1), None, ALU.min))
            link(v.tensor_tensor(blen[:], ps[0:1, 7, 128 + T:128 + 2 * T], brow[:, 0:T], ALU.subtract))
            link(v.tensor_tensor(cnt_cmp[:], blen[:].unsqueeze(2).broadcast_to([1, T, CP // U]),
                                 steps[:].unsqueeze(1).broadcast_to([1, T, CP // U]), ALU.is_gt))
            link(v.tensor_reduce(brow[:, T:2 * T], cnt_cmp[:], axis=AX.X, op=ALU.add))
            link(v.tensor_scalar(brow[:, T:2 * T], brow[:, T:2 * T], 1.0, None, ALU.max))
            link(v.tensor_scalar(blen[:], brow[:, T:2 * T], float(-U), float(CP), ALU.mult, ALU.add))
            link(v.tensor_tensor(brow[:, 0:T], brow[:, 0:T], blen[:], ALU.min))
            v.tensor_copy(brow_i[:], brow[:]).then_inc(s_brow, 1)
            dve.wait_ge(s_brow, 1)

            def windows(b):
                lo = dve.value_load(brow_i[0:1, b:b + 1], min_val=0, max_val=C - 1)
                n = dve.value_load(brow_i[0:1, T + b:T + b + 1], min_val=1, max_val=CP // U)
                if b >= 1:
                    dve.wait_ge(s_adj, b)
                with dve.Fori(0, n) as i:
                    c = nc.s_assert_within(lo + i * U, 0, CP - U,
                                           skip_runtime_bounds_check_because="lo + 11 n <= CP")
                    v.tensor_tensor(win[:, bass.ds(i * U, U), :],
                                    iota16[0:P, b * P:(b + 1) * P].unsqueeze(1).broadcast_to([P, U, P]),
                                    dcol[:, bass.ds(c, U)].unsqueeze(2).broadcast_to([P, U, P]), ALU.is_equal)
                v.memset(marks[:, b:b + 1], 0.0).then_inc(s_win, 1)

            def newton(n, m_):
                link(v.reciprocal(rstd[0:m_, 0:n], vroot[0:m_, 0:n]))
                link(v.tensor_tensor(vtmp[0:m_, 0:n], rstd[0:m_, 0:n], rstd[0:m_, 0:n], ALU.mult))
                link(v.tensor_tensor(vtmp[0:m_, 0:n], vtmp[0:m_, 0:n], veps[0:m_, 0:n], ALU.mult))
                link(v.tensor_scalar(vtmp[0:m_, 0:n], vtmp[0:m_, 0:n], -0.5, 1.5, ALU.mult, ALU.add))
                link(v.tensor_tensor(rstd[0:m_, 0:n], rstd[0:m_, 0:n], vtmp[0:m_, 0:n], ALU.mult))

            def layernorm(dst, src, roots, done):
                for t in range(T):
                    v.bn_stats(st6[0:P, t, :], src[:, t, :])
                link(v.memset(marks[:, T:T + 1], 0.0))
                for t in range(T):
                    v.bn_aggr(mv[0:P, t, :], st6[0:P, t, :])
                link(v.memset(marks[:, T:T + 1], 0.0))
                v.tensor_scalar(veps[0:P, :], mv[0:P, :, 1], EPS, None, ALU.add).then_inc(s_var, 1)
                dve.wait_ge(s_root, roots)
                newton(T, P)
                for t in range(T):
                    v.tensor_scalar(dst[:, t, :], src[:, t, :], mv[0:P, t, 0:1], rstd[0:P, t:t + 1],
                                    ALU.subtract, ALU.mult).then_inc(done, 1)

            windows(0)
            sources(FIRST, CP)
            windows(1)
            dve.wait_ge(s_x, 16)
            layernorm(h0, x_sb, 1, s_h0)
            dve.wait_ge(s_vecT, 2)
            v.tensor_copy(vcols[:], ps[:, 6, 256:256 + 3 * (KH + KD)])
            link(v.tensor_scalar(eps1[:], ps[0:P, 6, 300:301], 1.0, None, ALU.add))
            dve.wait_ge(s_hi, 1)
            v.tensor_tensor(wr_lo[:], wr_f[:], wr_hi[:].bitcast(f32), ALU.subtract).then_inc(s_vecT, 1)

            def at_diag(b):
                dve.wait_ge(s_atc, 2 * b + 2)
                sl = aT[b % 2][:, b, :]
                v.scalar_tensor_tensor(sl, ident[0:P, 0:P], eps1[:], sl, ALU.mult, ALU.add).then_inc(s_at, 1)

            def agg_lo(b):
                dve.wait_ge(s_hhiT, b + 1)
                v.tensor_tensor(hT_lo[:, :, b * P:(b + 1) * P],
                                ps[:, 5, 0:KD * P].rearrange("p (k n) -> p k n", k=KD),
                                hT_hi[:, :, b * P:(b + 1) * P].bitcast(f32), ALU.subtract).then_inc(s_hT, 1)

            def split_lo(slot, i, buf):
                dve.wait_ge(s_hi, i + 2)
                v.tensor_tensor(wt_lo[buf][:], raw[slot][:], wt_hi[buf][:].bitcast(f32),
                                ALU.subtract).then_inc(s_lo, 1)

            dve.wait_ge(s_pre, 48)
            v.memset(hT_hi[:, :, N:NP].bitcast(f32), 0.0)
            v.memset(hT_lo[:, :, N:NP].bitcast(f32), 0.0)
            for b in range(2, T):
                windows(b)
                at_diag(b - 2)
                if b >= 3:
                    agg_lo(b - 3)
            at_diag(T - 2)
            agg_lo(T - 3)
            at_diag(T - 1)
            v.tensor_tensor(x_sb[:], x_sb[:], h0[:], ALU.add).then_inc(s_v, 1)
            n_v[0] += 1
            split_lo(0, 0, 0)
            agg_lo(T - 2)
            split_lo(1, 1, 1)
            agg_lo(T - 1)
            split_lo(2, 2, 2)

            def bn_stats_of(z, i):
                dve.wait_ge(s_zc, i + 1)
                v.bn_stats(st6[:, 0, :], z[:, 0:HALF])
                link(v.bn_stats(st6[:, 1, :], z[:, HALF:N]))
                link(v.bn_aggr(mv[:, 0, :], st6[:, 0:2, :].rearrange("p a b -> p (a b)")))
                v.tensor_scalar(veps[:, 0:1], mv[:, 0, 1:2], EPS, None, ALU.add).then_inc(s_var, 1)

            def bn_scale(i, gam, bet):
                dve.wait_ge(s_root, i + 2)
                newton(1, 128)
                link(v.tensor_tensor(bscale[:, i:i + 1], rstd[:, 0:1], vcols[:, gam:gam + 1], ALU.mult))
                link(v.tensor_tensor(vtmp[:, 0:1], mv[:, 0, 0:1], bscale[:, i:i + 1], ALU.mult))
                v.tensor_tensor(bshift[:, i:i + 1], vcols[:, bet:bet + 1], vtmp[:, 0:1], ALU.subtract).then_inc(s_sc, 1)

            bn_stats_of(zb[:, 0, :], 0)
            for f in range(KH):
                bn_scale(f, KH + f, 2 * KH + f)
                if f + 1 < KH:
                    bn_stats_of(zb[:, (f + 1) % 2, :], f + 1)
                dve.wait_ge(s_rhi, f + 1)
                v.tensor_tensor(r1_lo[:, f, :], zb[:, f % 2, :], r1_hi[:, f, :].bitcast(f32),
                                ALU.subtract).then_inc(s_rlo, 1)
                if f == 4:
                    split_lo(3, 3, 0)
            split_lo(4, 4, G_)

            def x1_piece(d):
                q = 4 + 2 * (d % 2)
                dve.wait_ge(s_h2T, d + 1)
                v.tensor_tensor(x_sb[:, 0:4, d * 128:(d + 1) * 128], x_sb[:, 0:4, d * 128:(d + 1) * 128],
                                ps[0:P, q, :].rearrange("p (t n) -> p t n", t=4), ALU.add)
                v.tensor_tensor(x_sb[:, 4, d * 128:(d + 1) * 128], x_sb[:, 4, d * 128:(d + 1) * 128],
                                ps[0:P, q + 1, 0:128], ALU.add).then_inc(s_x1, 1)

            bn_stats_of(z2[:, 0, :], KH)
            for d in range(KD):
                bn_scale(KH + d, 3 * KH + KD + d, 3 * KH + 2 * KD + d)
                if d + 1 < KD:
                    bn_stats_of(z2[:, d + 1, :], KH + d + 1)
                if d >= 1:
                    x1_piece(d - 1)
            x1_piece(KD - 1)
            dve.wait_ge(s_x1, KD)
            layernorm(xn, x_sb, 2 + KH + KD, s_xn)
            split_lo(5, 5, U_)
            v.memset(xnT_hi[:, :, N:NP].bitcast(f32), 0.0)
            v.memset(xnT_lo[:, :, N:NP].bitcast(f32), 0.0)
            for t in range(T):
                dve.wait_ge(s_xnhi, t + 1)
                v.tensor_tensor(xnT_lo[:, :, t * P:(t + 1) * P],
                                ps[:, t % 2, 0:KD * P].rearrange("p (k n) -> p k n", k=KD),
                                xnT_hi[:, :, t * P:(t + 1) * P].bitcast(f32), ALU.subtract).then_inc(s_xnlo, 1)
            dve.wait_ge(s_xn, T)
            v.tensor_tensor(x_sb[:], x_sb[:], xn[:], ALU.add).then_inc(s_acc, 1)
            split_lo(0, 6, D_)
            dve.wait_ge(s_lg, 1)
            link(v.tensor_reduce(psum1[:, 2, :], ps[0:P, 4, 0:T * E].rearrange("p (t e) -> p t e", t=T),
                                 axis=AX.X, op=ALU.max))
            v.tensor_scalar(psum1[:, 0, :], psum1[:, 2, :], -1.0, None, ALU.mult).then_inc(s_nmx, 1)

            def route_top():
                dve.wait_ge(s_exp, T)
                link(v.reciprocal(psum1[:, 2, :], psum1[:, 1, :]))
                link(v.tensor_tensor(prob[:], prob[:], psum1[:, 2, :].unsqueeze(2).broadcast_to([P, T, E]), ALU.mult))
                for t in range(T):
                    v.max(top8[:, t, :], prob[:, t, :])
                link(v.memset(marks[:, T:T + 1], 0.0))
                for t in range(T):
                    v.max_index(top8i[:, t, :], top8[:, t, :], prob[:, t, :])
                link(v.tensor_reduce(psum1[:, 3, :], top8[:, :, 0:TOPK], axis=AX.X, op=ALU.add))
                link(v.reciprocal(psum1[:, 4, :], psum1[:, 3, :]))
                v.tensor_tensor(pair[:, :, 1].rearrange("p (k t) -> p k t", t=T),
                                top8[:, :, 0:TOPK].rearrange("p t k -> p k t"),
                                psum1[:, 4, :].unsqueeze(1).broadcast_to([P, TOPK, T]), ALU.mult)
                link(v.tensor_copy(top8f[:], top8i[:]))

            def route_mask():
                dve.wait_ge(s_cst, 16)
                link(v.tensor_tensor(ohk[:], iota64[0:P, :].unsqueeze(1).unsqueeze(1).broadcast_to([P, TOPK, T, E]),
                                     top8f[:, :, 0:TOPK].rearrange("p t k -> p k t").unsqueeze(3)
                                     .broadcast_to([P, TOPK, T, E]), ALU.is_equal))
                with nc.allow_low_precision(reason="sums of zeros and at most a single one"):
                    v.tensor_reduce(maskb[:], ohk[:].rearrange("p k t e -> p t e k"), axis=AX.X,
                                    op=ALU.add).then_inc(s_mask, 1)

            def route_dest():
                dve.wait_ge(s_pos, 1)
                link(v.tensor_tensor(slotv[:], ps[0:P, 6, 0:T * E].rearrange("p (t e) -> p t e", t=T),
                                     rowoff[0:P, :].unsqueeze(1).broadcast_to([P, T, E]), ALU.add))
                for k in range(TOPK):
                    v.tensor_tensor(prod[:, k, :, :], ohk[:, k, :, :], slotv[:], ALU.mult)
                link(v.memset(marks[:, T:T + 1], 0.0))
                link(v.tensor_reduce(dest[:], prod[:], axis=AX.X, op=ALU.add))
                v.tensor_copy(dest_i[:], dest[:].rearrange("p k t -> p (k t)")).then_inc(s_dest, 1)

            def route_extra():
                cnt = ps[:, 7, 0:E]
                link(v.tensor_scalar(extra[:], cnt, float(CAP), None, ALU.is_gt))
                for k in range(2, TILES):
                    link(v.scalar_tensor_tensor(extra[:], cnt, float(CAP * k), extra[:], ALU.is_gt, ALU.add))
                link(v.memset(one64[:], 1.0))
                link(v.tensor_tensor_scan(incl[:], one64[:], extra[:], 0.0, ALU.mult, ALU.add))
                link(v.tensor_scalar(cmp64[:], incl[:], pidx[:], None, ALU.is_le))
                link(v.tensor_tensor(prod64[:], cmp64[:], extra[:], ALU.mult))
                v.tensor_reduce(ocol[:, 2:3], prod64[:], axis=AX.X, op=ALU.add)
                link(v.tensor_reduce(ocol[:, 3:4], cmp64[:], axis=AX.X, op=ALU.add))
                link(v.tensor_scalar(ocol[:, 0:1], ocol[:, 3:4], float(E - 1), None, ALU.min))
                link(v.tensor_tensor(ocol[:, 4:5], pidx[:], ocol[:, 2:3], ALU.subtract))
                link(v.tensor_scalar(ocol[:, 4:5], ocol[:, 4:5], float(CAP), float(CAP), ALU.mult, ALU.add))
                v.scalar_tensor_tensor(ocol[:, 1:2], ocol[:, 3:4], float(ROWS), ocol[:, 4:5],
                                       ALU.mult, ALU.add).then_inc(s_ovc, 1)

            def route_rows():
                dve.wait_ge(s_ovT, 1)
                v.tensor_copy(ovrow[:, 0:2 * MAXOV], ps[0:1, 4, 0:2 * MAXOV])
                link(v.tensor_copy(ovrow[:, 2 * MAXOV:2 * MAXOV + 1], incl[0:1, E - 1:E]))
                v.memset(marks[:, T + 1:T + 2], 0.0).then_inc(s_ov, 1)

            def route_index():
                dve.wait_ge(s_lstT, 1)
                link(v.tensor_copy(gate_sb[:], ps[0:CAP, 4, E:2 * E]))
                v.tensor_copy(idx_sb[:], ps[0:CAP, 4, 0:E]).then_inc(s_idx, 1)

            def mult(J, h, m_):
                dve.wait_ge(s_silu, J + 1)
                dve.wait_ge(s_u, J + 1)
                v.tensor_tensor(hs[h][0:m_, :], hs[h][0:m_, :], ps[0:m_, 1, :], ALU.mult).then_inc(s_mul, 1)

            def h_lo(J, m_):
                dve.wait_ge(s_hhi, J + 1)
                v.tensor_tensor(hTj_lo[:, :, 0:m_], ps[:, 3, 0:KD * m_].rearrange("p (k n) -> p k n", k=KD),
                                hTj_hi[:, :, 0:m_].bitcast(f32), ALU.subtract).then_inc(s_hlo, 1)

            def y_add(q):
                dve.wait_ge(s_d, q + 1)
                if q == 0:
                    dve.wait_ge(s_acc, 1)
                if q >= T:
                    dve.wait_ge(s_y, q - T + 1)
                v.tensor_tensor(x_sb[:, q % T, :], x_sb[:, q % T, :], ps[0:P, 2, :], ALU.add).then_inc(s_y, 1)

            plan = {0: route_top, 1: route_mask, 2: route_dest, 3: route_extra, 5: route_rows, 9: route_index}
            for q in range(NSH):
                if q == T - 1:
                    split_lo(7 % NR, 7, G_)
                if q >= 1:
                    h_lo(q - 1, P)
                if q == T - 1:
                    split_lo(8 % NR, 8, U_)
                if q == 9:
                    route_index()
                    split_lo(ITEM0 % NR, ITEM0, G_)
                mult(q, q % 2, P)
                if q >= 1:
                    y_add(q - 1)
                if q == T:
                    split_lo(9 % NR, 9, D_)
                if q < 9 and q in plan:
                    plan[q]()

            def x_lo(j, h):
                dve.wait_ge(s_xhi, j + 1)
                v.tensor_tensor(xT_lo[h][:], ps[:, 5, 0:KD * CAP].rearrange("p (k n) -> p k n", k=KD),
                                xT_hi[h][:].bitcast(f32), ALU.subtract).then_inc(s_xlo, 1)

            x_lo(0, 0)
            split_lo((ITEM0 + 1) % NR, ITEM0 + 1, U_)
            h_lo(NSH - 1, P)
            y_add(NSH - 1)

            def step(j, h, hn, first_=False, last_=False):
                J = j + NSH
                if not first_:
                    h_lo(J - 1, CAP)
                if not last_:
                    x_lo(j + 1, hn)
                    b0 = ITEM0 - 1 + 3 * (1 + h)
                    i = item_of(0, j + 1)
                    split_lo(b0 % NR, i, G_)
                    mult(J, h, CAP)
                    split_lo((b0 + 1) % NR, i + 1, U_)
                    split_lo((b0 + 2) % NR, i + 2, D_)
                else:
                    mult(J, h, CAP)
                    split_lo((ITEMS - 1) % NR, ITEMS - 1, D_)

            step(0, 0, 1, first_=True)
            with dve.Fori(0, PAIRS) as i:
                step(i * 2 + 1, 1, 0)
                step(i * 2 + 2, 0, 1)
            step(E - 1, 1, 0, last_=True)
            h_lo(NSH + E - 1, CAP)
            total = dve.value_load(ovrow[0:1, 2 * MAXOV:2 * MAXOV + 1], min_val=0, max_val=MAXOV)
            with dve.If(total > 0):
                with dve.Fori(0, total) as o:
                    dve.wait_ge(s_lc, o * 16 + 16)
                    dve.wait_ge(s_scat, o * 16 + 16 * E)
                    v.tensor_copy(lidx[:], lcol[:, 0:1]).then_inc(s_li, 1)
                    for r, buf in enumerate((G_, U_, D_)):
                        split_lo(r, o * 3 + (ITEMS + r), buf)
                    x_lo(o + E, 0)
                    mult(o + (NSH + E), 0, CAP)
                    h_lo(o + (NSH + E), CAP)

        @block.tensor
        def _(pe):
            t_ = nc.tensor
            pe.wait_ge(s_cst, 3)
            pe.wait_ge(s_edgef, 2)
            t_.transpose(ps[0:P, 6, 0:C], dstf[:], ident[0:C, 0:C])
            t_.transpose(ps[0:P, 6, C:2 * C], srcf[:], ident[0:C, 0:C]).then_inc(s_edgeT, 1)
            pe.wait_ge(s_bnd, 2)
            t_.transpose(ps[0:2 * T, 7, 0:C], bounds[:], ident[0:C, 0:C]).then_inc(s_bndT, 1)
            pe.wait_ge(s_bmx, 1)
            t_.transpose(ps[0:1, 7, 128:128 + 2 * T], bmax[:], ident[0:2 * T, 0:2 * T]).then_inc(s_bmxT, 1)
            NV = 3 * (KH + KD)
            pe.wait_ge(s_vec, 96)
            pe.wait_ge(s_eps, 16)
            pe.wait_ge(s_oh, 1)
            t_.transpose(ps[:, 6, 256:256 + NV], vrows[:], ident[0:NV, 0:NV]).then_inc(s_vecT, 1)
            t_.matmul(ps[0:P, 6, 300:301], ones_row[:], eps_sb[:], start=True, stop=True).then_inc(s_vecT, 1)

            pe.wait_ge(s_brow, 1)

            def adjacency(b):
                q = 2 * (b % 2)
                outs = ((ps[0:P, q, 0:4 * P], 0, 4 * P), (ps[0:P, q + 1, 0:P], 4 * P, N))
                lo = pe.value_load(brow_i[0:1, b:b + 1], min_val=0, max_val=C - 1)
                n = pe.value_load(brow_i[0:1, T + b:T + b + 1], min_val=1, max_val=CP // U)
                pe.wait_ge(s_win, b + 1)
                if b == 0:
                    need = nc.s_assert_within(lo + n * U, 1, CP,
                                              skip_runtime_bounds_check_because="lo + 11 n <= CP")
                    pe.wait_ge(s_oh, need)
                if b == 1:
                    pe.wait_ge(s_oh, CP)
                if b >= 2:
                    pe.wait_ge(s_ac, 2 * b - 2)
                for o, c0, c1 in outs:
                    t_.matmul(o, zero_b[:], oh[:, 0, c0:c1], start=True, stop=False)
                with pe.Fori(0, n) as i:
                    for u in range(U):
                        c = nc.s_assert_within(lo + i * U + u, u, CP - U + u,
                                               skip_runtime_bounds_check_because="lo + 11 n <= CP")
                        for o, c0, c1 in outs:
                            t_.matmul(o, win[:, i * U + u, :], oh[:, c, c0:c1], start=False, stop=False)
                for o, c0, c1 in outs:
                    last = t_.matmul(o, zero_b[:], oh[:, 0, c0:c1], start=False, stop=True)
                last.then_inc(s_adj, 1)

            def a_transpose(b):
                pe.wait_ge(s_ac, 2 * b + 2)
                if b >= 1:
                    pe.wait_ge(s_atc, 2 * b)
                for s in range(T):
                    o = ps[0:P, 4, s * P:(s + 1) * P] if s < 4 else ps[0:P, 7, 0:P]
                    last = t_.transpose(o, ablk[:, s * P:(s + 1) * P], ident[0:P, 0:P])
                last.then_inc(s_aT, 1)

            def aggregate(b):
                pe.wait_ge(s_at, b + 1)
                pe.wait_ge(s_h0, T)
                if b >= 1:
                    pe.wait_ge(s_hT, b)
                for d in range(KD):
                    for s in range(T):
                        last = t_.matmul(ps[:, 5, d * P:(d + 1) * P], h0[:, s, d * 128:(d + 1) * 128],
                                         aT[b % 2][:, s, :], start=(s == 0), stop=(s == T - 1))
                last.then_inc(s_agg, 1)

            for b in range(T):
                adjacency(b)
                if b >= 1:
                    a_transpose(b - 1)
                if b >= 2:
                    aggregate(b - 2)
            a_transpose(T - 1)
            aggregate(T - 2)
            aggregate(T - 1)

            def split_product(outs, terms):
                n = len(terms)
                for k, (ah, al, bh, bl) in enumerate(terms):
                    for p_, (a, b) in enumerate(((ah, bh), (ah, bl), (al, bh))):
                        for o, r in zip(outs, b):
                            last = t_.matmul(o, a, r, start=(k == 0 and p_ == 0), stop=(k == n - 1 and p_ == 2))
                return last

            def halves(t, k):
                return [t[:, k, 0:HALF], t[:, k, HALF:NP]]

            for f in range(KH):
                buf = f // 4
                if f == 0:
                    pe.wait_ge(s_hT, T)
                pe.wait_ge(s_lo, buf + 1)
                if f >= 2:
                    pe.wait_ge(s_zc, f - 1)
                q = 2 * (f % 2)
                col = (f % 4) * 128
                split_product([ps[:, q, 0:HALF], ps[:, q + 1, 0:HALF]],
                              [(wt_hi[buf][:, k, col:col + 128], wt_lo[buf][:, k, col:col + 128],
                                halves(hT_hi, k), halves(hT_lo, k)) for k in range(KD)]).then_inc(s_z, 1)

            def h2_transpose(d):
                q = 4 + 2 * (d % 2)
                pe.wait_ge(s_r, KH + d + 1)
                if d >= 2:
                    pe.wait_ge(s_x1, d - 1)
                for t in range(T):
                    last = t_.transpose(ps[0:P, q + t // 4, (t % 4) * 128:(t % 4 + 1) * 128],
                                        z2[:, d, t * P:(t + 1) * P], ident[:])
                last.then_inc(s_h2T, 1)

            for d in range(KD):
                i = KH + d
                if d == 0:
                    pe.wait_ge(s_lo, 4)
                    pe.wait_ge(s_rlo, KH)
                pe.wait_ge(s_zc, i - 1)
                q = 2 * (i % 2)
                col = d * 128
                split_product([ps[:, q, 0:HALF], ps[:, q + 1, 0:HALF]],
                              [(wt_hi[2 if k < KD else 0][:, k % KD, col:col + 128],
                                wt_lo[2 if k < KD else 0][:, k % KD, col:col + 128],
                                halves(r1_hi, k), halves(r1_lo, k)) for k in range(KH)]).then_inc(s_z, 1)
                if d >= 1:
                    h2_transpose(d - 1)
            h2_transpose(KD - 1)
            pe.wait_ge(s_zc, KH + KD)
            for t in range(T):
                pe.wait_ge(s_xn, t + 1)
                if t >= 2:
                    pe.wait_ge(s_xnlo, t - 1)
                for k in range(KD):
                    last = t_.transpose(ps[:, t % 2, k * P:(k + 1) * P], xn[:, t, k * 128:(k + 1) * 128],
                                        ident[0:P, 0:P])
                last.then_inc(s_xnp, 1)
            pe.wait_ge(s_xnlo, T)
            pe.wait_ge(s_x1, KD)
            pe.wait_ge(s_vecT, 3)
            split_product([ps[0:E, 2, 0:HALF], ps[0:E, 3, 0:HALF]],
                          [(wr_hi[:, k, :], wr_lo[:, k, :], halves(xnT_hi, k), halves(xnT_lo, k))
                           for k in range(KD)]).then_inc(s_lgT, 1)
            pe.wait_ge(s_lgTc, 1)
            for t in range(T):
                last = t_.transpose(ps[0:P, 4, t * E:(t + 1) * E], lgT[:, t * P:(t + 1) * P], ident[0:E, 0:E])
            last.then_inc(s_lg, 1)

            def product(bank, m_, lhi, llo, buf, done):
                split_product([ps[0:m_, bank, :]],
                              [(lhi(k), llo(k), [wt_hi[buf][:, k, :]], [wt_lo[buf][:, k, :]])
                               for k in range(KD)]).then_inc(done, 1)

            def gate(J, m_, lhi, llo):
                if not isinstance(J, int) or J >= 1:
                    pe.wait_ge(s_silu, J)
                product(0, m_, lhi, llo, G_, s_g)

            def up(J, m_, lhi, llo):
                if not isinstance(J, int) or J >= 1:
                    pe.wait_ge(s_mul, J)
                product(1, m_, lhi, llo, U_, s_u)

            def h_transpose(J, h, m_):
                pe.wait_ge(s_mul, J + 1)
                if not isinstance(J, int) or J >= 1:
                    pe.wait_ge(s_hlo, J)
                for k in range(KD):
                    last = t_.transpose(ps[:, 3, k * m_:(k + 1) * m_], hs[h][0:m_, k * 128:(k + 1) * 128],
                                        ident[0:m_, 0:m_])
                last.then_inc(s_th, 1)

            def down(J, m_):
                pe.wait_ge(s_hlo, J + 1)
                if not isinstance(J, int) or J >= 1:
                    pe.wait_ge(s_y, J)
                product(2, m_, lambda k: hTj_hi[:, k, 0:m_], lambda k: hTj_lo[:, k, 0:m_], D_, s_d)

            def positions():
                pe.wait_ge(s_mask, 1)
                for t in range(T):
                    for s in range(t + 1):
                        last = t_.matmul(ps[0:P, 6, t * E:(t + 1) * E], before[:] if s == t else ones_b[:, 0:P],
                                         maskb[:, s, :], start=(s == 0), stop=(s == t))
                for s in range(T):
                    last = t_.matmul(ps[:, 7, 0:E], ones_b[:], maskb[:, s, :], start=(s == 0), stop=(s == T - 1))
                last.then_inc(s_pos, 1)

            def extra_rows():
                pe.wait_ge(s_ovc, 1)
                pe.wait_ge(s_exp, T)
                for r in range(2):
                    last = t_.transpose(ps[0:1, 4, r * MAXOV:(r + 1) * MAXOV], ocol[:, r:r + 1], ident[:])
                last.then_inc(s_ovT, 1)

            def list_columns():
                pe.wait_ge(s_lst, 16)
                pe.wait_ge(s_ov, 1)
                for r in range(2):
                    last = t_.transpose(ps[0:CAP, 4, r * E:(r + 1) * E], ltile[:, :, r], ident[0:E, 0:E])
                last.then_inc(s_lstT, 1)

            def x_transpose(j, h, use):
                pe.wait_ge(s_xg[h], use)
                if not isinstance(j, int) or j >= 1:
                    pe.wait_ge(s_xlo, j)
                for k in range(KD):
                    last = t_.transpose(ps[:, 5, k * CAP:(k + 1) * CAP], xg[h][:, k * 128:(k + 1) * 128],
                                        ident[0:CAP, 0:CAP])
                last.then_inc(s_tx, 1)

            for q in range(NSH):
                n0 = (q % T) * P
                lhi = lambda k: xnT_hi[:, k, n0:n0 + P]
                llo = lambda k: xnT_lo[:, k, n0:n0 + P]
                if q == 0:
                    pe.wait_ge(s_lo, 5)
                if q == T:
                    pe.wait_ge(s_lo, 8)
                gate(q, P, lhi, llo)
                if q >= 1:
                    h_transpose(q - 1, (q - 1) % 2, P)
                if q == 0:
                    pe.wait_ge(s_lo, 6)
                if q == T:
                    pe.wait_ge(s_lo, 9)
                up(q, P, lhi, llo)
                if q >= 1:
                    if q == 1:
                        pe.wait_ge(s_lo, 7)
                    if q == T + 1:
                        pe.wait_ge(s_lo, 10)
                    down(q - 1, P)
                if q == 1:
                    positions()
                if q == 4:
                    extra_rows()
                if q == 8:
                    list_columns()
            x_transpose(0, 0, 16)
            h_transpose(NSH - 1, (NSH - 1) % 2, P)
            down(NSH - 1, P)

            def step(j, h, hn, xuse, first_=False, last_=False):
                J = j + NSH
                i = item_of(0, j)
                if first_:
                    pe.wait_ge(s_lo, ITEM0 + 1)
                else:
                    pe.wait_ge(s_lo, i + 1)
                if first_:
                    pe.wait_ge(s_xlo, 1)
                else:
                    pe.wait_ge(s_xlo, j + 1)
                lhi = lambda k: xT_hi[h][:, k, :]
                llo = lambda k: xT_lo[h][:, k, :]
                gate(J, CAP, lhi, llo)
                if not first_:
                    h_transpose(J - 1, hn, CAP)
                if not last_:
                    x_transpose(j + 1, hn, xuse)
                if first_:
                    pe.wait_ge(s_lo, ITEM0 + 2)
                else:
                    pe.wait_ge(s_lo, i + 2)
                up(J, CAP, lhi, llo)
                if not first_:
                    pe.wait_ge(s_lo, i + 3)
                    down(J - 1, CAP)

            step(0, 0, 1, 16, first_=True)
            with pe.Fori(0, PAIRS) as i:
                step(i * 2 + 1, 1, 0, i * 16 + 32)
                step(i * 2 + 2, 0, 1, i * 16 + 32)
            step(E - 1, 1, 0, None, last_=True)
            h_transpose(NSH + E - 1, 1, CAP)
            pe.wait_ge(s_lo, ITEMS)
            down(NSH + E - 1, CAP)
            total = pe.value_load(ovrow[0:1, 2 * MAXOV:2 * MAXOV + 1], min_val=0, max_val=MAXOV)
            with pe.If(total > 0):
                with pe.Fori(0, total) as o:
                    x_transpose(o + E, 0, o * 16 + 16 * (E // 2 + 1))
                    pe.wait_ge(s_xlo, o + (E + 1))
                    pe.wait_ge(s_lo, o * 3 + (ITEMS + 3))
                    lhi = lambda k: xT_hi[0][:, k, :]
                    llo = lambda k: xT_lo[0][:, k, :]
                    gate(o + (NSH + E), CAP, lhi, llo)
                    up(o + (NSH + E), CAP, lhi, llo)
                    h_transpose(o + (NSH + E), 0, CAP)
                    down(o + (NSH + E), CAP)


_INS = ['x', 'src', 'dst', 'L0_gnn_eps', 'L0_gnn_W1', 'L0_gnn_b1', 'L0_gnn_g1', 'L0_gnn_be1', 'L0_gnn_W2',
        'L0_gnn_b2', 'L0_gnn_g2', 'L0_gnn_be2', 'L0_ffn_Wr', 'L0_ffn_sWg', 'L0_ffn_sWu', 'L0_ffn_sWd',
        'L0_ffn_Wg', 'L0_ffn_Wu', 'L0_ffn_Wd']


def kernel(**inputs):
    import numpy as _np
    import concourse.bacc as _bacc
    from concourse import mybir as _mybir
    from concourse.bass_utils import run_bass_kernel_spmd as _run

    nc = _bacc.Bacc("TRN2", target_bir_lowering=False, num_devices=1)
    arrays, args = {}, []
    for name in _INS:
        a = _np.ascontiguousarray(inputs[name])
        if a.ndim == 0 or name == 'L0_gnn_eps':
            a = a.reshape(1, 1)
        arrays[f"in_{name}"] = a
        args.append(nc.dram_tensor(f"in_{name}", a.shape, _mybir.dt.from_np(a.dtype), kind="ExternalInput").ap())
    n, d = inputs['x'].shape
    args.append(nc.dram_tensor("out_0", (n, d), _mybir.dt.float32, kind="ExternalOutput").ap())
    gnn_moe_kernel(nc, *args)
    r = _run(nc, [arrays], core_ids=[0])
    return r.results[0]["out_0"]
```

```python
import concourse.bass as bass
from concourse import mybir
from contextlib import ExitStack

f32 = mybir.dt.float32
f32r = mybir.dt.float32r
bf16 = mybir.dt.bfloat16
i16 = mybir.dt.int16
i32 = mybir.dt.int32
u32 = mybir.dt.uint32
ALU = mybir.AluOpType
ACT = mybir.ActivationFunctionType
AX = mybir.AxisListType


def gnn_moe_kernel(nc, x_in, src_in, dst_in, eps_in, W1, b1, g1, be1, W2, b2, g2, be2,
                   Wr, sWg, sWu, sWd, Wg, Wu, Wd, out):
    N, D = x_in.shape
    NE = src_in.shape[0]
    H = W1.shape[1]
    E = Wg.shape[0]
    NS = sWg.shape[0]
    TOPK = 6
    EPS = 1e-5
    P = 125
    T = N // P
    C = NE // P
    assert N == T * P and NE == C * P and D == 512 and H == 2 * D and E == 64
    KD = D // 128
    KH = H // 128
    U = 11
    CP = -(-C // U) * U
    HALF = 314
    NP = 2 * HALF
    CAP = 88
    TILES = -(-N // CAP)
    ROWS = TILES * CAP
    DUMMY = N
    TAB = DUMMY + CAP
    MAXOV = 128
    NR = 9
    NSH = NS * T
    ITEM0 = 4 + 3 * NS
    ITEMS = ITEM0 + 3 * E

    ctx = ExitStack()
    with ctx:
        base = [-(-nc.sbuf_base // 64) * 64]

        def region(size):
            at = base[0]
            base[0] = at + -(-size // 64) * 64
            assert base[0] <= nc.sbuf_usable_end, base[0]
            return at

        class Region:
            def __init__(self, size):
                self.start, self.end = region(size), 0
                self.end = base[0]
                self.at = self.start

            def rewind(self):
                self.at = self.start

            def place(self, name, shape, dt):
                n = mybir.dt.size(dt)
                for s in shape[1:]:
                    n *= s
                t = nc.alloc_sbuf_tensor_at(name, shape, dt, offset=self.at)
                self.at += -(-n // 32) * 32
                assert self.at <= self.end, (name, self.at - self.end)
                return t

        rMisc = Region(11136)
        rX = Region(T * D * 4)
        rH0 = Region(T * D * 4)
        rAT = Region(T * N * 4)
        rHT = Region(2 * KD * NP * 4 + 64)
        rRaw = Region(2 * 8192)
        rWin = Region(CP * P * 2)
        rOh = Region(CP * N * 2)

        m = rMisc.place
        ident = m("ident", [128, 128], f32)
        iota16 = m("iota16", [128, N], i16)
        vrows = m("vrows", [3 * (KH + KD), 128], f32)
        vcols = m("vcols", [128, 3 * (KH + KD)], f32)
        ones_b = m("ones_b", [P, 128], bf16)
        zero_b = m("zero_b", [P, P], bf16)
        before = m("before", [P, P], bf16)
        ones_row = m("ones_row", [1, P], f32)
        eps_sb = m("eps_sb", [1, 1], f32)
        eps1 = m("eps1", [P, 1], f32)
        pidx = m("pidx", [128, 1], f32)
        blk_lo = m("blk_lo", [128, T], f32)
        blk_hi = m("blk_hi", [128, T], f32)
        steps = m("steps", [1, CP // U], f32)
        cnt_cmp = m("cnt_cmp", [1, T, CP // U], f32)
        cmin = m("cmin", [C, 1], f32)
        cmax = m("cmax", [C, 1], f32)
        touch = m("touch", [C, T], f32)
        fromend = m("fromend", [C, 1], f32)
        after = m("after", [C, 1], f32)
        bounds = m("bounds", [C, 2 * T], f32)
        bmax = m("bmax", [2 * T, 1], f32)
        brow = m("brow", [1, 3 * T], f32)
        blen = m("blen", [1, T], f32)
        brow_i = m("brow_i", [1, 3 * T], i32)
        dcol = m("dcol", [P, CP], f32)
        scol = m("scol", [P, CP], f32)
        st6 = m("st6", [128, T, 6], f32)
        mv = m("mv", [128, T, 2], f32)
        veps = m("veps", [128, T], f32)
        vroot = m("vroot", [128, T], f32)
        rstd = m("rstd", [128, T], f32)
        vtmp = m("vtmp", [128, T], f32)
        marks = m("marks", [1, T + 2], f32)
        bscale = m("bscale", [128, KH + KD], f32)
        bshift = m("bshift", [128, KH + KD], f32)
        ovrow = m("ovrow", [1, 2 * MAXOV + 1], i32)
        lidx = m("lidx", [CAP, 1], i32)
        gidx = [m(f"gidx{i}", [CAP, 1], i32) for i in range(2)]
        sidx = [m(f"sidx{i}", [CAP, 1], i32) for i in range(2)]
        wr_f = m("wr_f", [128, KD, E], f32)
        wr_hi = m("wr_hi", [128, KD, E], f32r)
        wr_lo = m("wr_lo", [128, KD, E], f32r)

        x_sb = rX.place("x_sb", [P, T, D], f32)
        h0 = rH0.place("h0", [P, T, D], f32)
        rH0.rewind()
        xn = rH0.place("xn", [P, T, D], f32)
        rH0.rewind()
        raw7 = rH0.place("raw7", [128, KD, 512], f32)
        aT = [rAT.place(f"aT{i}", [P, T, P], f32) for i in range(2)]
        ablk = rAT.place("ablk", [P, N], f32)
        rAT.rewind()
        raw8 = rAT.place("raw8", [128, KD, 512], f32)
        rAT.rewind()
        lpre = rAT.place("lpre", [E, ROWS, 2], f32)
        rAT.rewind()
        zb = rAT.place("zb", [128, 2, NP], f32)
        rAT.rewind()
        z2 = rAT.place("z2", [128, KD, NP], f32)
        rAT.rewind()
        ohk = rAT.place("ohk", [P, TOPK, T, E], bf16)
        prod = rAT.place("prod", [P, TOPK, T, E], f32)
        ltile = rAT.place("ltile", [E, CAP, 2], f32)
        hT_hi = rHT.place("hT_hi", [128, KD, NP], f32r)
        hT_lo = rHT.place("hT_lo", [128, KD, NP], f32r)
        rHT.rewind()
        xnT_hi = rHT.place("xnT_hi", [128, KD, NP], f32r)
        xnT_lo = rHT.place("xnT_lo", [128, KD, NP], f32r)
        raw = [rRaw.place(f"raw{i}", [128, KD, 512], f32) for i in range(2)]
        win = rWin.place("win", [P, CP, P], bf16)
        rWin.rewind()
        r1_hi = rWin.place("r1_hi", [128, KH, NP], f32r)
        rWin.rewind()
        hs = [rWin.place(f"hs{i}", [128, D], f32) for i in range(2)]
        ysb = [rWin.place(f"ysb{i}", [CAP, D], f32) for i in range(2)]
        hTj_hi = rWin.place("hTj_hi", [128, KD, 128], f32r)
        hTj_lo = rWin.place("hTj_lo", [128, KD, 128], f32r)
        raw6 = rWin.place("raw6", [128, KD, 512], f32)
        oh = rOh.place("oh", [P, CP, N], bf16)
        rOh.rewind()
        raw += [rOh.place(f"raw{i}", [128, KD, 512], f32) for i in range(2, 6)]
        raw += [raw6, raw7, raw8]
        wt_hi = [rOh.place(f"wt_hi{i}", [128, KD, 512], f32r) for i in range(3)]
        wt_lo = [rOh.place(f"wt_lo{i}", [128, KD, 512], f32r) for i in range(3)]
        tail = rOh.at
        r1_lo = rOh.place("r1_lo", [128, KH, NP], f32r)
        rOh.at = tail
        xg = [rOh.place(f"xg{i}", [CAP, D], f32) for i in range(2)]
        xT_hi = [rOh.place(f"xT_hi{i}", [128, KD, CAP], f32r) for i in range(2)]
        xT_lo = [rOh.place(f"xT_lo{i}", [128, KD, CAP], f32r) for i in range(2)]
        lgT = rOh.place("lgT", [E, NP], f32)
        prob = rOh.place("prob", [P, T, E], f32)
        maskb = rOh.place("maskb", [P, T, E], bf16)
        slotv = rOh.place("slotv", [P, T, E], f32)
        top8 = rOh.place("top8", [P, T, 8], f32)
        top8i = rOh.place("top8i", [P, T, 8], u32)
        top8f = rOh.place("top8f", [P, T, 8], f32)
        psum1 = rOh.place("psum1", [P, 5, T], f32)
        dest = rOh.place("dest", [P, TOPK, T], f32)
        dest_i = rOh.place("dest_i", [P, TOPK * T], i32)
        pair = rOh.place("pair", [P, TOPK * T, 2], f32)
        extra = rOh.place("extra", [128, E], f32)
        incl = rOh.place("incl", [128, E], f32)
        one64 = rOh.place("one64", [128, E], f32)
        cmp64 = rOh.place("cmp64", [128, E], f32)
        prod64 = rOh.place("prod64", [128, E], f32)
        ocol = rOh.place("ocol", [128, 6], f32)
        idx_sb = rOh.place("idx_sb", [CAP, E], i32)
        gate_sb = rOh.place("gate_sb", [CAP, E], f32)
        lcol = rOh.place("lcol", [CAP, 2], f32)
        iota64 = rOh.place("iota64", [128, E], f32)
        rowoff = rOh.place("rowoff", [128, E], f32)
        rHT.rewind()
        src_i = rHT.place("src_i", [C, P], i32)
        dstf = rHT.place("dstf", [C, P], f32)
        srcf = rHT.place("srcf", [C, P], f32)
        zrows = rHT.place("zrows", [CAP, D], f32)
        dst_i = rHT.place("dst_i", [C, P], i32)

        ps = ctx.enter_context(nc.psum_tensor("ps", [128, 8, 512], f32))

        x_tab = nc.dram_tensor("x_tab", [TAB, D], f32, kind="Internal").ap()
        out_tab = nc.dram_tensor("out_tab", [TAB, D], f32, kind="Internal").ap()
        slots = nc.dram_tensor("slots", [E * ROWS, 2], f32, kind="Internal").ap()

        def sem(name):
            return ctx.enter_context(nc.semaphore(name))

        s_edges, s_x, s_vec, s_eps, s_wr = (sem(n) for n in
                                            ("edges_in", "x_in", "vectors_in", "eps_in", "router_in"))
        s_raw = [sem(f"raw_in{i}") for i in range(NR)]
        s_pre = sem("prefilled")
        s_cst = sem("constants")
        s_v = sem("vector_step")
        s_a = sem("scalar_step")
        s_edgef, s_edgeT, s_bnd, s_bndT, s_bmx, s_bmxT, s_brow = (sem(n) for n in (
            "edges_float", "edges_T", "bounds", "bounds_T", "bounds_max", "bounds_row_T", "block_rows"))
        s_vecT, s_oh, s_win, s_adj, s_atc, s_at, s_h0 = (sem(n) for n in (
            "vectors_T", "onehot_src", "windows", "adjacency", "aT_copied", "aT_ready", "h0_ready"))
        s_ac, s_aT = sem("A_copied"), sem("A_transposed")
        s_agg, s_hhiT, s_hT = (sem(n) for n in ("aggregated", "hT_hi_ready", "hT_ready"))
        s_var, s_root = sem("variance"), sem("root")
        s_z, s_zc, s_sc, s_r, s_rhi, s_rlo = (sem(n) for n in (
            "z_product", "z_copied", "bn_scale", "relu_done", "relu_hi", "relu_lo"))
        s_h2T, s_x1 = sem("h2_T"), sem("x1_piece")
        s_xn, s_xnp, s_xnhi, s_xnlo = sem("xn_tile"), sem("xn_T"), sem("xnT_hi"), sem("xnT_lo")
        s_xtab, s_lgT, s_lgTc, s_lg = sem("x_tab_out"), sem("logits_T"), sem("logits_T_copied"), sem("logits")
        s_nmx, s_exp, s_mask, s_pos, s_dest = (sem(n) for n in ("neg_max", "exps", "mask", "positions", "dest"))
        s_sct, s_lst, s_lstT, s_idx = (sem(n) for n in ("slots_out", "slots_in", "slots_T", "index_ready"))
        s_ovc, s_ovT, s_ov = sem("extra_cols"), sem("extra_T"), sem("extra_ready")
        s_acc = sem("base_sum")
        s_hi, s_lo = sem("weights_hi"), sem("weights_lo")
        s_g, s_u, s_th, s_d, s_tx = (sem(n) for n in ("gate_product", "up_product", "h_T", "down_product", "x_T"))
        s_silu, s_mul, s_hhi, s_hlo, s_y = (sem(n) for n in ("silu_done", "h_done", "h_hi", "h_lo", "y_ready"))
        s_xg = [sem(f"x_gathered{i}") for i in range(2)]
        s_xhi, s_xlo = sem("x_hi"), sem("x_lo")
        s_col = sem("index_column")
        s_go = sem("indirect_let_through")
        s_tab, s_scat, s_lc, s_li, s_out = (sem(n) for n in (
            "out_tab_base", "y_added", "extra_slots_in", "extra_index", "out_done"))

        W1v = W1.rearrange("(k p) n -> p k n", p=128)
        W2v = W2.rearrange("(k p) n -> p k n", p=128)
        first = [W1v[:, :, 0:512], W1v[:, :, 512:1024], W2v[:, 0:KD, :], W2v[:, KD:KH, :]]
        for s in range(NS):
            first += [w[s].rearrange("(k p) n -> p k n", p=128) for w in (sWg, sWu, sWd)]
        experts = [w.rearrange("e (k p) n -> e p k n", p=128) for w in (Wg, Wu, Wd)]
        G_, U_, D_ = 1, 2, 0

        PAIRS = (E - 2) // 2
        SIX = 6
        ROUNDS = (E - 4) // SIX
        assert 3 * SIX % NR == 0 and SIX % 2 == 0 and ROUNDS * SIX == E - 4
        uses = [len([i for i in range(ITEMS) if i % NR == s]) for s in range(NR)]

        def item_of(r, j):
            return ITEM0 + 3 * j - 1 + r

        def slot_of(r, j):
            return item_of(r, j) % NR

        def count_of(r, j, i=None):
            first_round = 16 * (item_of(r, j) // NR + 1)
            return first_round if i is None else i * (16 * 3 * SIX // NR) + first_round

        block = ctx.enter_context(nc.Block())

        @block.sync
        def _(sp):
            sp.dma_start(dst_i[:], dst_in.rearrange("(c p) -> c p", p=P)).then_inc(s_edges, 16)
            sp.dma_start(src_i[:], src_in.rearrange("(c p) -> c p", p=P)).then_inc(s_edges, 16)
            sp.dma_start(x_sb[:], x_in.rearrange("(t p) d -> p t d", p=P)).then_inc(s_x, 16)
            for i in range(2):
                sp.dma_start(raw[i][:], first[i]).then_inc(s_raw[i], 16)
            sp.wait_ge(s_adj, T)
            for i in range(2, ITEM0):
                if i >= NR:
                    sp.wait_ge(s_lo, i - NR + 1)
                if i == 6:
                    sp.wait_ge(s_z, KH + KD)
                if i == 7:
                    sp.wait_ge(s_acc, 1)
                    sp.wait_ge(s_xtab, 16)
                if i == 8:
                    sp.wait_ge(s_dest, 1)
                sp.dma_start(raw[i % NR][:], first[i]).then_inc(s_raw[i % NR], 16)
            for r, i in ((0, ITEM0), (1, ITEM0 + 1)):
                sp.wait_ge(s_lo, i - NR + 1)
                sp.dma_start(raw[i % NR][:], experts[r][0]).then_inc(s_raw[i % NR], 16)

            def load_step(j, c):
                for r in range(3):
                    slot = slot_of(r, c)
                    sp.wait_ge(s_lo, item_of(r, j) - NR + 1)
                    sp.dma_start(raw[slot][:], experts[r][j if r < 2 else j - 1]).then_inc(s_raw[slot], 16)

            for j in range(1, 4):
                load_step(j, j)
            with sp.Fori(0, ROUNDS) as i:
                for c in range(4, 4 + SIX):
                    load_step(i * SIX + c, c)
            sp.wait_ge(s_lo, ITEMS - NR)
            sp.dma_start(raw[(ITEMS - 1) % NR][:], experts[2][E - 1]).then_inc(s_raw[(ITEMS - 1) % NR], 16)
            sp.wait_ge(s_ov, 1)
            total = sp.value_load(ovrow[0:1, 2 * MAXOV:2 * MAXOV + 1], min_val=0, max_val=MAXOV)
            with sp.If(total > 0):
                with sp.Fori(0, total) as o:
                    e = sp.value_load(ovrow[0:1, bass.ds(o, 1)], min_val=0, max_val=E - 1)
                    sp.wait_ge(s_lo, o * 3 + ITEMS)
                    for r in range(3):
                        sp.dma_start(raw[r][:], experts[r][e]).then_inc(s_raw[r], 16)
            sp.wait_ge(s_scat, total * 16 + 16 * E)
            sp.dma_start(out.rearrange("(a b) d -> a (b d)", b=5), out_tab[0:N, :].rearrange("(a b) d -> a (b d)", b=5)).then_inc(s_out, 16)
            sp.wait_ge(s_out, 16)

        @block.gpsimd
        def _(pool):
            g = nc.gpsimd
            g.iota(iota16[:], pattern=[[1, N]], base=0, channel_multiplier=0).then_inc(s_cst, 1)
            g.memset(ident[:], 0.0).then_inc(s_cst, 1)
            pool.wait_ge(s_cst, 2)
            g.affine_select(out=ident[:], in_=ident[:], compare_op=ALU.not_equal, fill=1.0, base=0,
                            pattern=[[-1, 128]], channel_multiplier=1).then_inc(s_cst, 1)
            imp = dict(allow_small_or_imprecise_dtypes=True)
            g.iota(pidx[:], pattern=[[0, 1]], base=0, channel_multiplier=1, **imp).then_inc(s_cst, 1)
            g.iota(blk_lo[:], pattern=[[P, T]], base=0, channel_multiplier=0, **imp).then_inc(s_cst, 1)
            g.iota(blk_hi[:], pattern=[[P, T]], base=P, channel_multiplier=0, **imp).then_inc(s_cst, 1)
            g.iota(steps[:], pattern=[[U, CP // U]], base=0, channel_multiplier=0, **imp).then_inc(s_cst, 1)
            g.memset(lpre[:], 0.0).then_inc(s_cst, 1)
            pool.wait_ge(s_cst, 8)
            g.iota(lpre[:, :, 0], pattern=[[0, TILES], [1, CAP]], base=DUMMY, channel_multiplier=0,
                   **imp).then_inc(s_cst, 1)
            g.memset(zrows[:], 0.0).then_inc(s_cst, 1)
            pool.wait_ge(s_cst, 10)
            g.dma_start(slots.rearrange("(e r) v -> e (r v)", r=ROWS),
                        lpre[:].rearrange("e r v -> e (r v)")).then_inc(s_pre, 16)
            g.dma_start(x_tab[DUMMY:TAB, :], zrows[:]).then_inc(s_pre, 16)
            g.dma_start(out_tab[DUMMY:TAB, :], zrows[:]).then_inc(s_pre, 16)
            g.memset(before[:], 1.0).then_inc(s_cst, 1)
            pool.wait_ge(s_cst, 11)
            g.affine_select(out=before[:], in_=before[:], compare_op=ALU.is_gt, fill=0.0, base=0,
                            pattern=[[1, P]], channel_multiplier=-1).then_inc(s_cst, 1)
            g.memset(ones_b[:], 1.0).then_inc(s_cst, 1)
            pool.wait_ge(s_xn, T)
            g.dma_start(x_tab[0:N, :].rearrange("(t p) d -> p t d", p=P), xn[:]).then_inc(s_xtab, 16)
            pool.wait_ge(s_z, KH + KD)
            g.iota(iota64[:], pattern=[[1, E]], base=0, channel_multiplier=0, **imp).then_inc(s_cst, 1)
            g.iota(rowoff[:], pattern=[[ROWS, E]], base=0, channel_multiplier=0, **imp).then_inc(s_cst, 1)
            g.iota(pair[:, :, 0].rearrange("p (k t) -> p k t", t=T), pattern=[[0, TOPK], [P, T]], base=0,
                   channel_multiplier=1, **imp).then_inc(s_cst, 1)
            pool.wait_ge(s_dest, 1)
            pool.wait_ge(s_cst, 16)
            pool.wait_ge(s_pre, 48)
            for n in range(TOPK * T):
                g.indirect_dma_start(out=slots, out_offset=bass.IndirectOffsetOnAxis(ap=dest_i[:, n:n + 1].bitcast(u32), axis=0),
                                     in_=pair[:, n, :], in_offset=None).then_inc(s_sct, 16)
            pool.wait_ge(s_sct, 16 * TOPK * T)
            g.dma_start(ltile[:], slots.rearrange("(e r) v -> e r v", r=ROWS)[:, 0:CAP, :]).then_inc(s_lst, 16)
            pool.wait_ge(s_xtab, 16)
            pool.wait_ge(s_idx, 1)

            def gather(j, h, copies):
                g.tensor_copy(gidx[h][:], idx_sb[:, bass.ds(j, 1)]).then_inc(s_col, 1)
                pool.wait_ge(s_col, copies)
                pool.sem_inc(s_go, 1)
                g.indirect_dma_start(out=xg[h][:], out_offset=None, in_=x_tab,
                                     in_offset=bass.IndirectOffsetOnAxis(ap=gidx[h][:].bitcast(u32), axis=0)
                                     ).then_inc(s_xg[h], 16)

            def scatter(j, h, copies):
                g.tensor_copy(sidx[h][:], idx_sb[:, bass.ds(j, 1)]).then_inc(s_col, 1)
                pool.wait_ge(s_col, copies)
                pool.wait_ge(s_y, j + (NSH + 1))
                if not isinstance(j, int) or j >= 1:
                    pool.wait_ge(s_scat, j * 16)
                pool.sem_inc(s_go, 1)
                g.indirect_dma_start(out=out_tab, out_offset=bass.IndirectOffsetOnAxis(ap=sidx[h][:].bitcast(u32), axis=0),
                                     in_=ysb[h][:], in_offset=None, compute_op=ALU.add).then_inc(s_scat, 16)

            gather(0, 0, 1)
            gather(1, 1, 2)
            pool.wait_ge(s_y, NSH)
            g.dma_start(out_tab[0:N, :].rearrange("(t p) d -> p t d", p=P), x_sb[:]).then_inc(s_tab, 16)
            pool.wait_ge(s_tab, 16)
            pool.wait_ge(s_tx, 1)
            gather(2, 0, 3)
            pool.wait_ge(s_tx, 2)
            gather(3, 1, 4)
            pool.wait_ge(s_tx, 3)
            gather(4, 0, 5)
            scatter(0, 0, 6)
            with pool.Fori(0, (E - 6) // 2) as i:
                for h in range(2):
                    pool.wait_ge(s_tx, i * 2 + (h + 4))
                    gather(i * 2 + (5 + h), 1 - h, i * 4 + (7 + 2 * h))
                    scatter(i * 2 + (1 + h), 1 - h, i * 4 + (8 + 2 * h))
            pool.wait_ge(s_tx, E - 2)
            gather(E - 1, 1, 2 * E - 5)
            for j in range(E - 5, E):
                scatter(j, j % 2, E + j + 1)
            pool.wait_ge(s_scat, 16 * E)
            pool.wait_ge(s_ov, 1)
            total = pool.value_load(ovrow[0:1, 2 * MAXOV:2 * MAXOV + 1], min_val=0, max_val=MAXOV)
            with pool.If(total > 0):
                with pool.Fori(0, total) as o:
                    at = pool.value_load(ovrow[0:1, bass.ds(o + MAXOV, 1)], min_val=0, max_val=E * ROWS - CAP)
                    g.dma_start(lcol[:], slots[bass.ds(at, CAP), :]).then_inc(s_lc, 16)
                    pool.wait_ge(s_li, o + 1)
                    pool.sem_inc(s_go, 1)
                    g.indirect_dma_start(out=xg[0][:], out_offset=None, in_=x_tab,
                                         in_offset=bass.IndirectOffsetOnAxis(ap=lidx[:, 0:1].bitcast(u32), axis=0)
                                         ).then_inc(s_xg[0], 16)
                    pool.wait_ge(s_y, o + (NSH + E + 1))
                    pool.sem_inc(s_go, 1)
                    g.indirect_dma_start(out=out_tab, out_offset=bass.IndirectOffsetOnAxis(ap=lidx[:, 0:1].bitcast(u32), axis=0),
                                         in_=ysb[0][:], in_offset=None, compute_op=ALU.add).then_inc(s_scat, 16)
                    pool.wait_ge(s_scat, o * 16 + 16 * (E + 1))

        @block.scalar
        def _(act):
            sc = nc.scalar
            at = 0
            for v, k in ((b1, KH), (g1, KH), (be1, KH), (b2, KD), (g2, KD), (be2, KD)):
                act.dma_start(vrows[at:at + k, :], v.rearrange("(k p) -> k p", p=128)).then_inc(s_vec, 16)
                at += k
            act.dma_start(eps_sb[:], eps_in).then_inc(s_eps, 16)
            act.dma_start(wr_f[:], Wr.rearrange("(k p) e -> p k e", p=128)).then_inc(s_wr, 16)
            act.wait_ge(s_wr, 16)
            sc.activation(wr_hi[:], wr_f[:], ACT.Copy).then_inc(s_hi, 1)

            def split_hi(slot, use, buf):
                act.wait_ge(s_raw[slot], use)
                sc.activation(wt_hi[buf][:], raw[slot][:], ACT.Copy).then_inc(s_hi, 1)

            def a_copy(b):
                act.wait_ge(s_adj, b + 1)
                if b == 0:
                    act.wait_ge(s_pre, 48)
                else:
                    act.wait_ge(s_aT, b)
                q = 2 * (b % 2)
                sc.activation(ablk[:, 0:4 * P], ps[0:P, q, 0:4 * P], ACT.Copy).then_inc(s_ac, 1)
                sc.activation(ablk[:, 4 * P:N], ps[0:P, q + 1, 0:P], ACT.Copy).then_inc(s_ac, 1)

            def at_copy(b):
                act.wait_ge(s_aT, b + 1)
                if b >= 2:
                    act.wait_ge(s_agg, b - 1)
                sc.activation(aT[b % 2][:, 0:4, :], ps[0:P, 4, 0:4 * P].rearrange("p (s n) -> p s n", s=4),
                              ACT.Copy).then_inc(s_atc, 1)
                sc.activation(aT[b % 2][:, 4, :], ps[0:P, 7, 0:P], ACT.Copy).then_inc(s_atc, 1)

            def agg_hi(b):
                act.wait_ge(s_agg, b + 1)
                sc.activation(hT_hi[:, :, b * P:(b + 1) * P],
                              ps[:, 5, 0:KD * P].rearrange("p (k n) -> p k n", k=KD), ACT.Copy).then_inc(s_hhiT, 1)

            a_copy(0)
            for b in range(1, T):
                a_copy(b)
                at_copy(b - 1)
                if b == 1:
                    act.wait_ge(s_var, 1)
                    sc.activation(vroot[0:P, :], veps[0:P, :], ACT.Sqrt).then_inc(s_root, 1)
                if b >= 2:
                    agg_hi(b - 2)
            at_copy(T - 1)
            split_hi(0, 16, 0)
            agg_hi(T - 2)
            split_hi(1, 16, 1)
            agg_hi(T - 1)
            split_hi(2, 16, 2)

            def z_copy(i, dst, bias):
                act.wait_ge(s_z, i + 1)
                q = 2 * (i % 2)
                sc.activation(dst.rearrange("p (h n) -> p h n", h=2), ps[:, q:q + 2, 0:HALF], ACT.Identity,
                              bias=vcols[:, bias:bias + 1]).then_inc(s_zc, 1)

            act.wait_ge(s_vecT, 2)
            act.wait_ge(s_at, T)
            act.wait_ge(s_agg, T)
            z_copy(0, zb[:, 0, :], 0)
            for f in range(KH):
                act.wait_ge(s_var, 2 + f)
                sc.activation(vroot[:, 0:1], veps[:, 0:1], ACT.Sqrt).then_inc(s_root, 1)
                if f + 1 < KH:
                    if f >= 1:
                        act.wait_ge(s_rlo, f)
                    z_copy(f + 1, zb[:, (f + 1) % 2, :], f + 1)
                act.wait_ge(s_sc, f + 1)
                sc.activation(zb[:, f % 2, :], zb[:, f % 2, :], ACT.Relu, bias=bshift[:, f:f + 1],
                              scale=bscale[:, f:f + 1]).then_inc(s_r, 1)
                act.wait_ge(s_r, f + 1)
                sc.activation(r1_hi[:, f, :], zb[:, f % 2, :], ACT.Copy).then_inc(s_rhi, 1)
                if f == 4:
                    act.wait_ge(s_z, 4)
                    split_hi(3, 16, 0)
            act.wait_ge(s_z, KH)
            split_hi(4, 16, G_)
            act.wait_ge(s_rlo, KH)
            z_copy(KH, z2[:, 0, :], 3 * KH)
            for d in range(KD):
                i = KH + d
                act.wait_ge(s_var, 2 + i)
                sc.activation(vroot[:, 0:1], veps[:, 0:1], ACT.Sqrt).then_inc(s_root, 1)
                if d + 1 < KD:
                    z_copy(i + 1, z2[:, d + 1, :], 3 * KH + d + 1)
                act.wait_ge(s_sc, i + 1)
                sc.activation(z2[:, d, :], z2[:, d, :], ACT.Relu, bias=bshift[:, i:i + 1],
                              scale=bscale[:, i:i + 1]).then_inc(s_r, 1)
            split_hi(5, 16, U_)
            split_hi(6, 16, D_)
            act.wait_ge(s_var, 2 + KH + KD)
            sc.activation(vroot[0:P, :], veps[0:P, :], ACT.Sqrt).then_inc(s_root, 1)
            for t in range(T):
                act.wait_ge(s_xnp, t + 1)
                sc.activation(xnT_hi[:, :, t * P:(t + 1) * P],
                              ps[:, t % 2, 0:KD * P].rearrange("p (k n) -> p k n", k=KD), ACT.Copy).then_inc(s_xnhi, 1)
            act.wait_ge(s_lgT, 1)
            sc.activation(lgT[:].rearrange("p (h n) -> p h n", h=2), ps[0:E, 2:4, 0:HALF], ACT.Copy).then_inc(s_lgTc, 1)
            act.wait_ge(s_nmx, 1)
            for t in range(T):
                sc.activation(prob[:, t, :], ps[0:P, 4, t * E:(t + 1) * E], ACT.Exp, bias=psum1[:, 0, t:t + 1],
                              accum_out=psum1[:, 1, t:t + 1]).then_inc(s_exp, 1)

            def silu(J, h, m_):
                act.wait_ge(s_g, J + 1)
                if not isinstance(J, int) or J >= 2:
                    act.wait_ge(s_th, J - 1)
                sc.activation(hs[h][0:m_, :], ps[0:m_, 0, :], ACT.Silu).then_inc(s_silu, 1)

            def h_hi(J, m_):
                act.wait_ge(s_th, J + 1)
                if not isinstance(J, int) or J >= 1:
                    act.wait_ge(s_d, J)
                sc.activation(hTj_hi[:, :, 0:m_], ps[:, 3, 0:KD * m_].rearrange("p (k n) -> p k n", k=KD),
                              ACT.Copy).then_inc(s_hhi, 1)

            for q in range(NSH):
                silu(q, q % 2, P)
                if q == T - 1:
                    split_hi(7, 16, G_)
                if q == NSH - 1:
                    split_hi(ITEM0 % NR, 32, G_)
                if q >= 1:
                    h_hi(q - 1, P)
                if q == T - 1:
                    act.wait_ge(s_u, T)
                    split_hi(8, 16, U_)
                if q == T:
                    act.wait_ge(s_d, T)
                    split_hi(0, 32, D_)
                if q == NSH - 1:
                    act.wait_ge(s_u, NSH)
                    split_hi((ITEM0 + 1) % NR, 32, U_)
            def x_hi(j, h):
                act.wait_ge(s_tx, j + 1)
                if not isinstance(j, int) or j >= 2:
                    act.wait_ge(s_u, j + (NSH - 1))
                sc.activation(xT_hi[h][:], ps[:, 5, 0:KD * CAP].rearrange("p (k n) -> p k n", k=KD),
                              ACT.Copy).then_inc(s_xhi, 1)

            def y_copy(j, h, gate):
                act.wait_ge(s_d, j + (NSH + 1))
                if not isinstance(j, int) or j >= 2:
                    act.wait_ge(s_scat, j * 16 - 16)
                sc.activation(ysb[h][:], ps[0:CAP, 2, :], ACT.Copy, scale=gate).then_inc(s_y, 1)

            x_hi(0, 0)
            h_hi(NSH - 1, P)

            def step(j, c, i=None):
                J = j + NSH
                h = c % 2
                silu(J, h, CAP)
                if c > 0:
                    h_hi(J - 1, CAP)
                if c < E - 1:
                    x_hi(j + 1, 1 - h)
                    split_hi(slot_of(0, c + 1), count_of(0, c + 1, i), G_)
                    act.wait_ge(s_u, J + 1)
                    split_hi(slot_of(1, c + 1), count_of(1, c + 1, i), U_)
                    act.wait_ge(s_d, J)
                    split_hi(slot_of(2, c + 1), count_of(2, c + 1, i), D_)
                else:
                    act.wait_ge(s_d, J)
                    split_hi((ITEMS - 1) % NR, 16 * uses[(ITEMS - 1) % NR], D_)
                if c > 0:
                    y_copy(j - 1, 1 - h, gate_sb[:, bass.ds(j - 1, 1)])

            for j in range(3):
                step(j, j)
            with act.Fori(0, ROUNDS) as i:
                for c in range(3, 3 + SIX):
                    step(i * SIX + c, c, i)
            step(E - 1, E - 1)
            h_hi(NSH + E - 1, CAP)
            y_copy(E - 1, 1, gate_sb[:, E - 1:E])
            act.wait_ge(s_ov, 1)
            total = act.value_load(ovrow[0:1, 2 * MAXOV:2 * MAXOV + 1], min_val=0, max_val=MAXOV)
            with act.If(total > 0):
                with act.Fori(0, total) as o:
                    for r, buf in enumerate((G_, U_, D_)):
                        act.wait_ge(s_raw[r], o * 16 + 16 * (uses[r] + 1))
                        act.wait_ge(s_d, o + (NSH + E))
                        sc.activation(wt_hi[buf][:], raw[r][:], ACT.Copy).then_inc(s_hi, 1)
                    x_hi(o + E, 0)
                    silu(o + (NSH + E), 0, CAP)
                    h_hi(o + (NSH + E), CAP)
                    act.wait_ge(s_scat, o * 16 + 16 * E)
                    y_copy(o + E, 0, lcol[:, 1:2])

        @block.vector
        def _(dve):
            v = nc.vector
            n_v = [0]

            def link(ins):
                n_v[0] += 1
                ins.then_inc(s_v, 1)
                dve.wait_ge(s_v, n_v[0])

            v.memset(dcol[:], -1.0)
            v.memset(scol[:], -1.0)
            v.memset(zero_b[:], 0.0)
            link(v.memset(ones_row[:], 1.0))
            dve.wait_ge(s_edges, 32)
            v.tensor_copy(dstf[:], dst_i[:]).then_inc(s_edgef, 1)
            v.tensor_copy(srcf[:], src_i[:]).then_inc(s_edgef, 1)
            dve.wait_ge(s_edgef, 2)
            v.tensor_reduce(cmin[:], dstf[:], axis=AX.X, op=ALU.min)
            link(v.tensor_reduce(cmax[:], dstf[:], axis=AX.X, op=ALU.max))
            dve.wait_ge(s_cst, 7)
            link(v.tensor_scalar(touch[:], blk_hi[0:C, :], cmin[:], None, ALU.is_gt))
            link(v.scalar_tensor_tensor(touch[:], blk_lo[0:C, :], cmax[:], touch[:], ALU.is_le, ALU.mult))
            v.tensor_scalar(fromend[:], pidx[0:C, :], -1.0, float(C), ALU.mult, ALU.add)
            link(v.tensor_scalar(after[:], pidx[0:C, :], 1.0, None, ALU.add))
            v.tensor_scalar(bounds[:, 0:T], touch[:], fromend[:], None, ALU.mult).then_inc(s_bnd, 1)
            v.tensor_scalar(bounds[:, T:2 * T], touch[:], after[:], None, ALU.mult).then_inc(s_bnd, 1)
            dve.wait_ge(s_edgeT, 1)
            v.tensor_copy(dcol[:, 0:C], ps[0:P, 6, 0:C])
            link(v.tensor_copy(scol[:, 0:C], ps[0:P, 6, C:2 * C]))

            def sources(a, b):
                for c in range(a, b):
                    v.tensor_scalar(oh[:, c, :], iota16[0:P, :], scol[:, c:c + 1], None, ALU.is_equal).then_inc(s_oh, 1)

            FIRST = 2
            sources(0, 9)
            dve.wait_ge(s_bndT, 1)
            v.tensor_reduce(bmax[:], ps[0:2 * T, 7, 0:C], axis=AX.X, op=ALU.max).then_inc(s_bmx, 1)
            sources(9, FIRST * U)
            dve.wait_ge(s_bmxT, 1)
            link(v.tensor_scalar(brow[:, 0:T], ps[0:1, 7, 128:128 + T], -1.0, float(C), ALU.mult, ALU.add))
            link(v.tensor_scalar(brow[:, 0:T], brow[:, 0:T], float(C - 1), None, ALU.min))
            link(v.tensor_tensor(blen[:], ps[0:1, 7, 128 + T:128 + 2 * T], brow[:, 0:T], ALU.subtract))
            link(v.tensor_tensor(cnt_cmp[:], blen[:].unsqueeze(2).broadcast_to([1, T, CP // U]),
                                 steps[:].unsqueeze(1).broadcast_to([1, T, CP // U]), ALU.is_gt))
            link(v.tensor_reduce(brow[:, T:2 * T], cnt_cmp[:], axis=AX.X, op=ALU.add))
            link(v.tensor_scalar(brow[:, T:2 * T], brow[:, T:2 * T], 1.0, None, ALU.max))
            link(v.tensor_scalar(blen[:], brow[:, T:2 * T], float(-U), float(CP), ALU.mult, ALU.add))
            link(v.tensor_tensor(brow[:, 0:T], brow[:, 0:T], blen[:], ALU.min))
            link(v.tensor_scalar(blen[:], brow[:, T:2 * T], float(U), None, ALU.mult))
            link(v.tensor_tensor(blen[:], blen[:], brow[:, 0:T], ALU.add))
            link(v.tensor_tensor(cnt_cmp[:], blen[:].unsqueeze(2).broadcast_to([1, T, CP // U]),
                                 steps[:].unsqueeze(1).broadcast_to([1, T, CP // U]), ALU.is_gt))
            link(v.tensor_reduce(brow[:, 2 * T:3 * T], cnt_cmp[:], axis=AX.X, op=ALU.add))
            link(v.tensor_scalar(brow[:, 2 * T:3 * T], brow[:, 2 * T:3 * T], float(FIRST), None, ALU.max))
            for b in range(2 * T + 1, 3 * T):
                link(v.tensor_tensor(brow[:, b:b + 1], brow[:, b:b + 1], brow[:, b - 1:b], ALU.max))
            v.tensor_copy(brow_i[:], brow[:]).then_inc(s_brow, 1)
            dve.wait_ge(s_brow, 1)

            def more_sources(b):
                made = FIRST if b == 0 else dve.value_load(brow_i[0:1, 2 * T + b - 1:2 * T + b],
                                                           min_val=FIRST, max_val=CP // U)
                want = dve.value_load(brow_i[0:1, 2 * T + b:2 * T + b + 1], min_val=FIRST, max_val=CP // U)
                with dve.If(want > made):
                    with dve.Fori(0, want - made) as i:
                        for u in range(U):
                            c = nc.s_assert_within((i + made) * U + u, u, CP - U + u,
                                                   skip_runtime_bounds_check_because="groups made <= CP / U")
                            v.tensor_scalar(oh[:, bass.ds(c, 1), :].rearrange("p a n -> p (a n)"), iota16[0:P, :],
                                            scol[:, bass.ds(c, 1)], None, ALU.is_equal).then_inc(s_oh, 1)

            def windows(b):
                lo = dve.value_load(brow_i[0:1, b:b + 1], min_val=0, max_val=C - 1)
                n = dve.value_load(brow_i[0:1, T + b:T + b + 1], min_val=1, max_val=CP // U)
                if b >= 1:
                    dve.wait_ge(s_adj, b)
                with dve.Fori(0, n) as i:
                    c = nc.s_assert_within(lo + i * U, 0, CP - U,
                                           skip_runtime_bounds_check_because="lo + U n <= CP")
                    v.tensor_tensor(win[:, bass.ds(i * U, U), :],
                                    iota16[0:P, b * P:(b + 1) * P].unsqueeze(1).broadcast_to([P, U, P]),
                                    dcol[:, bass.ds(c, U)].unsqueeze(2).broadcast_to([P, U, P]),
                                    ALU.is_equal).then_inc(s_win, 1)

            def newton(n, m_):
                link(v.reciprocal(rstd[0:m_, 0:n], vroot[0:m_, 0:n]))
                link(v.tensor_tensor(vtmp[0:m_, 0:n], rstd[0:m_, 0:n], rstd[0:m_, 0:n], ALU.mult))
                link(v.tensor_tensor(vtmp[0:m_, 0:n], vtmp[0:m_, 0:n], veps[0:m_, 0:n], ALU.mult))
                link(v.tensor_scalar(vtmp[0:m_, 0:n], vtmp[0:m_, 0:n], -0.5, 1.5, ALU.mult, ALU.add))
                link(v.tensor_tensor(rstd[0:m_, 0:n], rstd[0:m_, 0:n], vtmp[0:m_, 0:n], ALU.mult))

            def layernorm(dst, src, roots, done):
                for t in range(T):
                    v.bn_stats(st6[0:P, t, :], src[:, t, :])
                link(v.memset(marks[:, T:T + 1], 0.0))
                for t in range(T):
                    v.bn_aggr(mv[0:P, t, :], st6[0:P, t, :])
                link(v.memset(marks[:, T:T + 1], 0.0))
                v.tensor_scalar(veps[0:P, :], mv[0:P, :, 1], EPS, None, ALU.add).then_inc(s_var, 1)
                dve.wait_ge(s_root, roots)
                newton(T, P)
                for t in range(T):
                    v.tensor_scalar(dst[:, t, :], src[:, t, :], mv[0:P, t, 0:1], rstd[0:P, t:t + 1],
                                    ALU.subtract, ALU.mult).then_inc(done, 1)

            windows(0)
            more_sources(0)
            more_sources(1)
            windows(1)
            more_sources(2)
            windows(2)
            dve.wait_ge(s_x, 16)
            layernorm(h0, x_sb, 1, s_h0)
            dve.wait_ge(s_vecT, 2)
            v.tensor_copy(vcols[:], ps[:, 6, 256:256 + 3 * (KH + KD)])
            link(v.tensor_scalar(eps1[:], ps[0:P, 6, 300:301], 1.0, None, ALU.add))
            dve.wait_ge(s_hi, 1)
            v.tensor_tensor(wr_lo[:], wr_f[:], wr_hi[:].bitcast(f32), ALU.subtract).then_inc(s_vecT, 1)

            def at_diag(b):
                dve.wait_ge(s_atc, 2 * b + 2)
                sl = aT[b % 2][:, b, :]
                v.scalar_tensor_tensor(sl, ident[0:P, 0:P], eps1[:], sl, ALU.mult, ALU.add).then_inc(s_at, 1)

            def agg_lo(b):
                dve.wait_ge(s_hhiT, b + 1)
                v.tensor_tensor(hT_lo[:, :, b * P:(b + 1) * P],
                                ps[:, 5, 0:KD * P].rearrange("p (k n) -> p k n", k=KD),
                                hT_hi[:, :, b * P:(b + 1) * P].bitcast(f32), ALU.subtract).then_inc(s_hT, 1)

            def split_lo(slot, i, buf):
                dve.wait_ge(s_hi, i + 2)
                v.tensor_tensor(wt_lo[buf][:], raw[slot][:], wt_hi[buf][:].bitcast(f32),
                                ALU.subtract).then_inc(s_lo, 1)

            dve.wait_ge(s_pre, 48)
            v.memset(hT_hi[:, :, N:NP].bitcast(f32), 0.0)
            v.memset(hT_lo[:, :, N:NP].bitcast(f32), 0.0)
            for b in range(2, T):
                if b >= 3:
                    more_sources(b)
                    windows(b)
                at_diag(b - 2)
                if b >= 3:
                    agg_lo(b - 3)
            v.tensor_tensor(x_sb[:], x_sb[:], h0[:], ALU.add).then_inc(s_v, 1)
            n_v[0] += 1
            at_diag(T - 2)
            agg_lo(T - 3)
            at_diag(T - 1)
            split_lo(0, 0, 0)
            agg_lo(T - 2)
            split_lo(1, 1, 1)
            agg_lo(T - 1)
            split_lo(2, 2, 2)

            def bn_stats_of(z, i):
                dve.wait_ge(s_zc, i + 1)
                v.bn_stats(st6[:, 0, :], z[:, 0:HALF])
                link(v.bn_stats(st6[:, 1, :], z[:, HALF:N]))
                link(v.bn_aggr(mv[:, 0, :], st6[:, 0:2, :].rearrange("p a b -> p (a b)")))
                v.tensor_scalar(veps[:, 0:1], mv[:, 0, 1:2], EPS, None, ALU.add).then_inc(s_var, 1)

            def bn_scale(i, gam, bet):
                dve.wait_ge(s_root, i + 2)
                newton(1, 128)
                link(v.tensor_tensor(bscale[:, i:i + 1], rstd[:, 0:1], vcols[:, gam:gam + 1], ALU.mult))
                link(v.tensor_tensor(vtmp[:, 0:1], mv[:, 0, 0:1], bscale[:, i:i + 1], ALU.mult))
                v.tensor_tensor(bshift[:, i:i + 1], vcols[:, bet:bet + 1], vtmp[:, 0:1], ALU.subtract).then_inc(s_sc, 1)

            bn_stats_of(zb[:, 0, :], 0)
            for f in range(KH):
                bn_scale(f, KH + f, 2 * KH + f)
                if f + 1 < KH:
                    bn_stats_of(zb[:, (f + 1) % 2, :], f + 1)
                dve.wait_ge(s_rhi, f + 1)
                v.tensor_tensor(r1_lo[:, f, :], zb[:, f % 2, :], r1_hi[:, f, :].bitcast(f32),
                                ALU.subtract).then_inc(s_rlo, 1)
                if f == 4:
                    split_lo(3, 3, 0)
            split_lo(4, 4, G_)

            def x1_piece(d):
                q = 4 + 2 * (d % 2)
                dve.wait_ge(s_h2T, d + 1)
                v.tensor_tensor(x_sb[:, 0:4, d * 128:(d + 1) * 128], x_sb[:, 0:4, d * 128:(d + 1) * 128],
                                ps[0:P, q, :].rearrange("p (t n) -> p t n", t=4), ALU.add)
                v.tensor_tensor(x_sb[:, 4, d * 128:(d + 1) * 128], x_sb[:, 4, d * 128:(d + 1) * 128],
                                ps[0:P, q + 1, 0:128], ALU.add).then_inc(s_x1, 1)

            bn_stats_of(z2[:, 0, :], KH)
            for d in range(KD):
                bn_scale(KH + d, 3 * KH + KD + d, 3 * KH + 2 * KD + d)
                if d + 1 < KD:
                    bn_stats_of(z2[:, d + 1, :], KH + d + 1)
                if d >= 1:
                    x1_piece(d - 1)
            x1_piece(KD - 1)
            dve.wait_ge(s_x1, KD)
            layernorm(xn, x_sb, 2 + KH + KD, s_xn)
            split_lo(5, 5, U_)
            v.memset(xnT_hi[:, :, N:NP].bitcast(f32), 0.0)
            v.memset(xnT_lo[:, :, N:NP].bitcast(f32), 0.0)
            for t in range(T):
                dve.wait_ge(s_xnhi, t + 1)
                v.tensor_tensor(xnT_lo[:, :, t * P:(t + 1) * P],
                                ps[:, t % 2, 0:KD * P].rearrange("p (k n) -> p k n", k=KD),
                                xnT_hi[:, :, t * P:(t + 1) * P].bitcast(f32), ALU.subtract).then_inc(s_xnlo, 1)
            dve.wait_ge(s_xn, T)
            v.tensor_tensor(x_sb[:], x_sb[:], xn[:], ALU.add).then_inc(s_acc, 1)
            split_lo(6, 6, D_)
            dve.wait_ge(s_lg, 1)
            link(v.tensor_reduce(psum1[:, 2, :], ps[0:P, 4, 0:T * E].rearrange("p (t e) -> p t e", t=T),
                                 axis=AX.X, op=ALU.max))
            v.tensor_scalar(psum1[:, 0, :], psum1[:, 2, :], -1.0, None, ALU.mult).then_inc(s_nmx, 1)

            def route_top():
                dve.wait_ge(s_exp, T)
                link(v.reciprocal(psum1[:, 2, :], psum1[:, 1, :]))
                link(v.tensor_tensor(prob[:], prob[:], psum1[:, 2, :].unsqueeze(2).broadcast_to([P, T, E]), ALU.mult))
                for t in range(T):
                    v.max(top8[:, t, :], prob[:, t, :])
                link(v.memset(marks[:, T:T + 1], 0.0))
                for t in range(T):
                    v.max_index(top8i[:, t, :], top8[:, t, :], prob[:, t, :])
                link(v.tensor_reduce(psum1[:, 3, :], top8[:, :, 0:TOPK], axis=AX.X, op=ALU.add))
                link(v.reciprocal(psum1[:, 4, :], psum1[:, 3, :]))
                v.tensor_tensor(pair[:, :, 1].rearrange("p (k t) -> p k t", t=T),
                                top8[:, :, 0:TOPK].rearrange("p t k -> p k t"),
                                psum1[:, 4, :].unsqueeze(1).broadcast_to([P, TOPK, T]), ALU.mult)
                link(v.tensor_copy(top8f[:], top8i[:]))

            def route_mask():
                dve.wait_ge(s_cst, 16)
                link(v.tensor_tensor(ohk[:], iota64[0:P, :].unsqueeze(1).unsqueeze(1).broadcast_to([P, TOPK, T, E]),
                                     top8f[:, :, 0:TOPK].rearrange("p t k -> p k t").unsqueeze(3)
                                     .broadcast_to([P, TOPK, T, E]), ALU.is_equal))
                with nc.allow_low_precision(reason="sums of zeros and at most a single one"):
                    v.tensor_reduce(maskb[:], ohk[:].rearrange("p k t e -> p t e k"), axis=AX.X,
                                    op=ALU.add).then_inc(s_mask, 1)

            def route_dest():
                dve.wait_ge(s_pos, 1)
                link(v.tensor_tensor(slotv[:], ps[0:P, 6, 0:T * E].rearrange("p (t e) -> p t e", t=T),
                                     rowoff[0:P, :].unsqueeze(1).broadcast_to([P, T, E]), ALU.add))
                for k in range(TOPK):
                    v.tensor_tensor(prod[:, k, :, :], ohk[:, k, :, :], slotv[:], ALU.mult)
                link(v.memset(marks[:, T:T + 1], 0.0))
                link(v.tensor_reduce(dest[:], prod[:], axis=AX.X, op=ALU.add))
                v.tensor_copy(dest_i[:], dest[:].rearrange("p k t -> p (k t)")).then_inc(s_dest, 1)

            def route_extra():
                cnt = ps[:, 7, 0:E]
                link(v.tensor_scalar(extra[:], cnt, float(CAP), None, ALU.is_gt))
                for k in range(2, TILES):
                    link(v.scalar_tensor_tensor(extra[:], cnt, float(CAP * k), extra[:], ALU.is_gt, ALU.add))
                link(v.memset(one64[:], 1.0))
                link(v.tensor_tensor_scan(incl[:], one64[:], extra[:], 0.0, ALU.mult, ALU.add))
                link(v.tensor_scalar(cmp64[:], incl[:], pidx[:], None, ALU.is_le))
                link(v.tensor_tensor(prod64[:], cmp64[:], extra[:], ALU.mult))
                v.tensor_reduce(ocol[:, 2:3], prod64[:], axis=AX.X, op=ALU.add)
                link(v.tensor_reduce(ocol[:, 3:4], cmp64[:], axis=AX.X, op=ALU.add))
                link(v.tensor_scalar(ocol[:, 0:1], ocol[:, 3:4], float(E - 1), None, ALU.min))
                link(v.tensor_tensor(ocol[:, 4:5], pidx[:], ocol[:, 2:3], ALU.subtract))
                link(v.tensor_scalar(ocol[:, 4:5], ocol[:, 4:5], float(CAP), float(CAP), ALU.mult, ALU.add))
                v.scalar_tensor_tensor(ocol[:, 1:2], ocol[:, 3:4], float(ROWS), ocol[:, 4:5],
                                       ALU.mult, ALU.add).then_inc(s_ovc, 1)

            def route_rows():
                dve.wait_ge(s_ovT, 1)
                v.tensor_copy(ovrow[:, 0:2 * MAXOV], ps[0:1, 4, 0:2 * MAXOV])
                link(v.tensor_copy(ovrow[:, 2 * MAXOV:2 * MAXOV + 1], incl[0:1, E - 1:E]))
                v.memset(marks[:, T + 1:T + 2], 0.0).then_inc(s_ov, 1)

            def route_index():
                dve.wait_ge(s_lstT, 1)
                link(v.tensor_copy(gate_sb[:], ps[0:CAP, 4, E:2 * E]))
                v.tensor_copy(idx_sb[:], ps[0:CAP, 4, 0:E]).then_inc(s_idx, 1)

            def mult(J, h, m_):
                dve.wait_ge(s_silu, J + 1)
                dve.wait_ge(s_u, J + 1)
                v.tensor_tensor(hs[h][0:m_, :], hs[h][0:m_, :], ps[0:m_, 1, :], ALU.mult).then_inc(s_mul, 1)

            def h_lo(J, m_):
                dve.wait_ge(s_hhi, J + 1)
                v.tensor_tensor(hTj_lo[:, :, 0:m_], ps[:, 3, 0:KD * m_].rearrange("p (k n) -> p k n", k=KD),
                                hTj_hi[:, :, 0:m_].bitcast(f32), ALU.subtract).then_inc(s_hlo, 1)

            def y_add(q):
                dve.wait_ge(s_d, q + 1)
                if q == 0:
                    dve.wait_ge(s_acc, 1)
                if q >= T:
                    dve.wait_ge(s_y, q - T + 1)
                v.tensor_tensor(x_sb[:, q % T, :], x_sb[:, q % T, :], ps[0:P, 2, :], ALU.add).then_inc(s_y, 1)

            plan = {0: route_top, 1: route_mask, 2: route_dest, 3: route_extra, 5: route_rows, 8: route_index}
            for q in range(NSH):
                if q == T - 1:
                    split_lo(7, 7, G_)
                if q >= 1:
                    h_lo(q - 1, P)
                if q == T - 1:
                    split_lo(8, 8, U_)
                if q == NSH - 1:
                    split_lo(ITEM0 % NR, ITEM0, G_)
                mult(q, q % 2, P)
                if q >= 1:
                    y_add(q - 1)
                if q == T:
                    split_lo(0, 9, D_)
                if q in plan:
                    plan[q]()

            def x_lo(j, h):
                dve.wait_ge(s_xhi, j + 1)
                v.tensor_tensor(xT_lo[h][:], ps[:, 5, 0:KD * CAP].rearrange("p (k n) -> p k n", k=KD),
                                xT_hi[h][:].bitcast(f32), ALU.subtract).then_inc(s_xlo, 1)

            x_lo(0, 0)
            split_lo((ITEM0 + 1) % NR, ITEM0 + 1, U_)
            h_lo(NSH - 1, P)
            y_add(NSH - 1)

            def step(j, c):
                J = j + NSH
                h = c % 2
                if c > 0:
                    h_lo(J - 1, CAP)
                if c < E - 1:
                    x_lo(j + 1, 1 - h)
                    split_lo(slot_of(0, c + 1), item_of(0, j + 1), G_)
                    mult(J, h, CAP)
                    split_lo(slot_of(1, c + 1), item_of(1, j + 1), U_)
                    split_lo(slot_of(2, c + 1), item_of(2, j + 1), D_)
                else:
                    mult(J, h, CAP)
                    split_lo((ITEMS - 1) % NR, ITEMS - 1, D_)

            for j in range(3):
                step(j, j)
            with dve.Fori(0, ROUNDS) as i:
                for c in range(3, 3 + SIX):
                    step(i * SIX + c, c)
            step(E - 1, E - 1)
            h_lo(NSH + E - 1, CAP)
            total = dve.value_load(ovrow[0:1, 2 * MAXOV:2 * MAXOV + 1], min_val=0, max_val=MAXOV)
            with dve.If(total > 0):
                with dve.Fori(0, total) as o:
                    dve.wait_ge(s_lc, o * 16 + 16)
                    dve.wait_ge(s_scat, o * 16 + 16 * E)
                    v.tensor_copy(lidx[:], lcol[:, 0:1]).then_inc(s_li, 1)
                    for r, buf in enumerate((G_, U_, D_)):
                        split_lo(r, o * 3 + (ITEMS + r), buf)
                    x_lo(o + E, 0)
                    mult(o + (NSH + E), 0, CAP)
                    h_lo(o + (NSH + E), CAP)

        @block.tensor
        def _(pe):
            t_ = nc.tensor
            pe.wait_ge(s_cst, 3)
            pe.wait_ge(s_edgef, 2)
            t_.transpose(ps[0:P, 6, 0:C], dstf[:], ident[0:C, 0:C])
            t_.transpose(ps[0:P, 6, C:2 * C], srcf[:], ident[0:C, 0:C]).then_inc(s_edgeT, 1)
            pe.wait_ge(s_bnd, 2)
            t_.transpose(ps[0:2 * T, 7, 0:C], bounds[:], ident[0:C, 0:C]).then_inc(s_bndT, 1)
            pe.wait_ge(s_bmx, 1)
            t_.transpose(ps[0:1, 7, 128:128 + 2 * T], bmax[:], ident[0:2 * T, 0:2 * T]).then_inc(s_bmxT, 1)
            NV = 3 * (KH + KD)
            pe.wait_ge(s_vec, 96)
            pe.wait_ge(s_eps, 16)
            pe.wait_ge(s_oh, 1)
            t_.transpose(ps[:, 6, 256:256 + NV], vrows[:], ident[0:NV, 0:NV]).then_inc(s_vecT, 1)
            t_.matmul(ps[0:P, 6, 300:301], ones_row[:], eps_sb[:], start=True, stop=True).then_inc(s_vecT, 1)

            pe.wait_ge(s_brow, 1)

            before_b = [0]

            def adjacency(b):
                q = 2 * (b % 2)
                outs = ((ps[0:P, q, 0:4 * P], 0, 4 * P), (ps[0:P, q + 1, 0:P], 4 * P, N))
                lo = pe.value_load(brow_i[0:1, b:b + 1], min_val=0, max_val=C - 1)
                n = pe.value_load(brow_i[0:1, T + b:T + b + 1], min_val=1, max_val=CP // U)
                need = nc.s_assert_within(lo + n * U, 1, CP,
                                          skip_runtime_bounds_check_because="lo + U n <= CP")
                pe.wait_ge(s_oh, need)
                if b >= 2:
                    pe.wait_ge(s_ac, 2 * b - 2)
                for o, c0, c1 in outs:
                    t_.matmul(o, zero_b[:], oh[:, 0, c0:c1], start=True, stop=False)
                with pe.Fori(0, n) as i:
                    pe.wait_ge(s_win, i + before_b[0] + 1)
                    for u in range(U):
                        c = nc.s_assert_within(lo + i * U + u, u, CP - U + u,
                                               skip_runtime_bounds_check_because="lo + U n <= CP")
                        for o, c0, c1 in outs:
                            t_.matmul(o, win[:, i * U + u, :], oh[:, c, c0:c1], start=False, stop=False)
                for o, c0, c1 in outs:
                    last = t_.matmul(o, zero_b[:], oh[:, 0, c0:c1], start=False, stop=True)
                last.then_inc(s_adj, 1)
                before_b[0] = before_b[0] + n

            def a_transpose(b):
                pe.wait_ge(s_ac, 2 * b + 2)
                if b >= 1:
                    pe.wait_ge(s_atc, 2 * b)
                for s in range(T):
                    o = ps[0:P, 4, s * P:(s + 1) * P] if s < 4 else ps[0:P, 7, 0:P]
                    last = t_.transpose(o, ablk[:, s * P:(s + 1) * P], ident[0:P, 0:P])
                last.then_inc(s_aT, 1)

            def aggregate(b):
                pe.wait_ge(s_at, b + 1)
                pe.wait_ge(s_h0, T)
                if b >= 1:
                    pe.wait_ge(s_hT, b)
                for d in range(KD):
                    for s in range(T):
                        last = t_.matmul(ps[:, 5, d * P:(d + 1) * P], h0[:, s, d * 128:(d + 1) * 128],
                                         aT[b % 2][:, s, :], start=(s == 0), stop=(s == T - 1))
                last.then_inc(s_agg, 1)

            for b in range(T):
                adjacency(b)
                if b >= 1:
                    a_transpose(b - 1)
                if b >= 2:
                    aggregate(b - 2)
            a_transpose(T - 1)
            aggregate(T - 2)
            aggregate(T - 1)

            def split_product(outs, terms, relu=False):
                n = len(terms)
                for k, (ah, al, bh, bl) in enumerate(terms):
                    if relu:
                        pe.wait_ge(s_rlo, k + 1)
                        if k == KD:
                            pe.wait_ge(s_lo, 4)
                    for p_, (a, b) in enumerate(((ah, bh), (ah, bl), (al, bh))):
                        for o, r in zip(outs, b):
                            last = t_.matmul(o, a, r, start=(k == 0 and p_ == 0), stop=(k == n - 1 and p_ == 2))
                return last

            def halves(t, k):
                return [t[:, k, 0:HALF], t[:, k, HALF:NP]]

            for f in range(KH):
                buf = f // 4
                if f == 0:
                    pe.wait_ge(s_hT, T)
                pe.wait_ge(s_lo, buf + 1)
                if f >= 2:
                    pe.wait_ge(s_zc, f - 1)
                q = 2 * (f % 2)
                col = (f % 4) * 128
                split_product([ps[:, q, 0:HALF], ps[:, q + 1, 0:HALF]],
                              [(wt_hi[buf][:, k, col:col + 128], wt_lo[buf][:, k, col:col + 128],
                                halves(hT_hi, k), halves(hT_lo, k)) for k in range(KD)]).then_inc(s_z, 1)

            def h2_transpose(d):
                q = 4 + 2 * (d % 2)
                pe.wait_ge(s_r, KH + d + 1)
                if d >= 2:
                    pe.wait_ge(s_x1, d - 1)
                for t in range(T):
                    last = t_.transpose(ps[0:P, q + t // 4, (t % 4) * 128:(t % 4 + 1) * 128],
                                        z2[:, d, t * P:(t + 1) * P], ident[:])
                last.then_inc(s_h2T, 1)

            for d in range(KD):
                i = KH + d
                if d == 0:
                    pe.wait_ge(s_lo, 3)
                pe.wait_ge(s_zc, i - 1)
                q = 2 * (i % 2)
                col = d * 128
                split_product([ps[:, q, 0:HALF], ps[:, q + 1, 0:HALF]],
                              [(wt_hi[2 if k < KD else 0][:, k % KD, col:col + 128],
                                wt_lo[2 if k < KD else 0][:, k % KD, col:col + 128],
                                halves(r1_hi, k), halves(r1_lo, k)) for k in range(KH)],
                              relu=(d == 0)).then_inc(s_z, 1)
                if d >= 1:
                    h2_transpose(d - 1)
            h2_transpose(KD - 1)
            pe.wait_ge(s_zc, KH + KD)
            for t in range(T):
                pe.wait_ge(s_xn, t + 1)
                if t >= 2:
                    pe.wait_ge(s_xnlo, t - 1)
                for k in range(KD):
                    last = t_.transpose(ps[:, t % 2, k * P:(k + 1) * P], xn[:, t, k * 128:(k + 1) * 128],
                                        ident[0:P, 0:P])
                last.then_inc(s_xnp, 1)
            pe.wait_ge(s_xnlo, T)
            pe.wait_ge(s_x1, KD)
            pe.wait_ge(s_vecT, 3)
            split_product([ps[0:E, 2, 0:HALF], ps[0:E, 3, 0:HALF]],
                          [(wr_hi[:, k, :], wr_lo[:, k, :], halves(xnT_hi, k), halves(xnT_lo, k))
                           for k in range(KD)]).then_inc(s_lgT, 1)
            pe.wait_ge(s_lgTc, 1)
            for t in range(T):
                last = t_.transpose(ps[0:P, 4, t * E:(t + 1) * E], lgT[:, t * P:(t + 1) * P], ident[0:E, 0:E])
            last.then_inc(s_lg, 1)

            def product(bank, m_, lhi, llo, buf, done):
                split_product([ps[0:m_, bank, :]],
                              [(lhi(k), llo(k), [wt_hi[buf][:, k, :]], [wt_lo[buf][:, k, :]])
                               for k in range(KD)]).then_inc(done, 1)

            def gate(J, m_, lhi, llo):
                if not isinstance(J, int) or J >= 1:
                    pe.wait_ge(s_silu, J)
                product(0, m_, lhi, llo, G_, s_g)

            def up(J, m_, lhi, llo):
                if not isinstance(J, int) or J >= 1:
                    pe.wait_ge(s_mul, J)
                product(1, m_, lhi, llo, U_, s_u)

            def h_transpose(J, h, m_):
                pe.wait_ge(s_mul, J + 1)
                if not isinstance(J, int) or J >= 1:
                    pe.wait_ge(s_hlo, J)
                for k in range(KD):
                    last = t_.transpose(ps[:, 3, k * m_:(k + 1) * m_], hs[h][0:m_, k * 128:(k + 1) * 128],
                                        ident[0:m_, 0:m_])
                last.then_inc(s_th, 1)

            def down(J, m_):
                pe.wait_ge(s_hlo, J + 1)
                if not isinstance(J, int) or J >= 1:
                    pe.wait_ge(s_y, J)
                product(2, m_, lambda k: hTj_hi[:, k, 0:m_], lambda k: hTj_lo[:, k, 0:m_], D_, s_d)

            def positions():
                pe.wait_ge(s_mask, 1)
                for t in range(T):
                    for s in range(t + 1):
                        last = t_.matmul(ps[0:P, 6, t * E:(t + 1) * E], before[:] if s == t else ones_b[:, 0:P],
                                         maskb[:, s, :], start=(s == 0), stop=(s == t))
                for s in range(T):
                    last = t_.matmul(ps[:, 7, 0:E], ones_b[:], maskb[:, s, :], start=(s == 0), stop=(s == T - 1))
                last.then_inc(s_pos, 1)

            def extra_rows():
                pe.wait_ge(s_ovc, 1)
                pe.wait_ge(s_exp, T)
                for r in range(2):
                    last = t_.transpose(ps[0:1, 4, r * MAXOV:(r + 1) * MAXOV], ocol[:, r:r + 1], ident[:])
                last.then_inc(s_ovT, 1)

            def list_columns():
                pe.wait_ge(s_lst, 16)
                pe.wait_ge(s_ov, 1)
                for r in range(2):
                    last = t_.transpose(ps[0:CAP, 4, r * E:(r + 1) * E], ltile[:, :, r], ident[0:E, 0:E])
                last.then_inc(s_lstT, 1)

            def x_transpose(j, h, use):
                pe.wait_ge(s_xg[h], use)
                if not isinstance(j, int) or j >= 1:
                    pe.wait_ge(s_xlo, j)
                for k in range(KD):
                    last = t_.transpose(ps[:, 5, k * CAP:(k + 1) * CAP], xg[h][:, k * 128:(k + 1) * 128],
                                        ident[0:CAP, 0:CAP])
                last.then_inc(s_tx, 1)

            for q in range(NSH):
                n0 = (q % T) * P
                lhi = lambda k: xnT_hi[:, k, n0:n0 + P]
                llo = lambda k: xnT_lo[:, k, n0:n0 + P]
                if q == 0:
                    pe.wait_ge(s_lo, 5)
                if q == T:
                    pe.wait_ge(s_lo, 8)
                gate(q, P, lhi, llo)
                if q >= 1:
                    h_transpose(q - 1, (q - 1) % 2, P)
                if q == 0:
                    pe.wait_ge(s_lo, 6)
                if q == T:
                    pe.wait_ge(s_lo, 9)
                up(q, P, lhi, llo)
                if q >= 1:
                    if q == 1:
                        pe.wait_ge(s_lo, 7)
                    if q == T + 1:
                        pe.wait_ge(s_lo, 10)
                    down(q - 1, P)
                if q == 1:
                    positions()
                if q == 4:
                    extra_rows()
                if q == 7:
                    list_columns()
            x_transpose(0, 0, 16)
            h_transpose(NSH - 1, (NSH - 1) % 2, P)
            down(NSH - 1, P)

            def step(j, h, hn, xuse, first_=False, last_=False):
                J = j + NSH
                i = item_of(0, j)
                if first_:
                    pe.wait_ge(s_lo, ITEM0 + 1)
                else:
                    pe.wait_ge(s_lo, i + 1)
                if first_:
                    pe.wait_ge(s_xlo, 1)
                else:
                    pe.wait_ge(s_xlo, j + 1)
                lhi = lambda k: xT_hi[h][:, k, :]
                llo = lambda k: xT_lo[h][:, k, :]
                gate(J, CAP, lhi, llo)
                if not first_:
                    h_transpose(J - 1, hn, CAP)
                if not last_:
                    x_transpose(j + 1, hn, xuse)
                if first_:
                    pe.wait_ge(s_lo, ITEM0 + 2)
                else:
                    pe.wait_ge(s_lo, i + 2)
                up(J, CAP, lhi, llo)
                if not first_:
                    pe.wait_ge(s_lo, i + 3)
                    down(J - 1, CAP)

            step(0, 0, 1, 16, first_=True)
            with pe.Fori(0, PAIRS) as i:
                step(i * 2 + 1, 1, 0, i * 16 + 32)
                step(i * 2 + 2, 0, 1, i * 16 + 32)
            step(E - 1, 1, 0, None, last_=True)
            h_transpose(NSH + E - 1, 1, CAP)
            pe.wait_ge(s_lo, ITEMS)
            down(NSH + E - 1, CAP)
            total = pe.value_load(ovrow[0:1, 2 * MAXOV:2 * MAXOV + 1], min_val=0, max_val=MAXOV)
            with pe.If(total > 0):
                with pe.Fori(0, total) as o:
                    x_transpose(o + E, 0, o * 16 + 16 * (E // 2 + 1))
                    pe.wait_ge(s_xlo, o + (E + 1))
                    pe.wait_ge(s_lo, o * 3 + (ITEMS + 3))
                    lhi = lambda k: xT_hi[0][:, k, :]
                    llo = lambda k: xT_lo[0][:, k, :]
                    gate(o + (NSH + E), CAP, lhi, llo)
                    up(o + (NSH + E), CAP, lhi, llo)
                    h_transpose(o + (NSH + E), 0, CAP)
                    down(o + (NSH + E), CAP)


_INS = ['x', 'src', 'dst', 'L0_gnn_eps', 'L0_gnn_W1', 'L0_gnn_b1', 'L0_gnn_g1', 'L0_gnn_be1', 'L0_gnn_W2',
        'L0_gnn_b2', 'L0_gnn_g2', 'L0_gnn_be2', 'L0_ffn_Wr', 'L0_ffn_sWg', 'L0_ffn_sWu', 'L0_ffn_sWd',
        'L0_ffn_Wg', 'L0_ffn_Wu', 'L0_ffn_Wd']


def kernel(**inputs):
    import numpy as _np
    import concourse.bacc as _bacc
    from concourse import mybir as _mybir
    from concourse.bass_utils import run_bass_kernel_spmd as _run

    nc = _bacc.Bacc("TRN2", target_bir_lowering=False, num_devices=1)
    arrays, args = {}, []
    for name in _INS:
        a = _np.ascontiguousarray(inputs[name])
        if a.ndim == 0 or name == 'L0_gnn_eps':
            a = a.reshape(1, 1)
        arrays[f"in_{name}"] = a
        args.append(nc.dram_tensor(f"in_{name}", a.shape, _mybir.dt.from_np(a.dtype), kind="ExternalInput").ap())
    n, d = inputs['x'].shape
    args.append(nc.dram_tensor("out_0", (n, d), _mybir.dt.float32, kind="ExternalOutput").ap())
    gnn_moe_kernel(nc, *args)
    r = _run(nc, [arrays], core_ids=[0])
    return r.results[0]["out_0"]
```
